# Optimizing a Trainium2 kernel written in Bass

```python
import numpy as np
import jax
import jax.numpy as jnp

def _softmax(x, axis=-1):
    return jax.nn.softmax(x, axis=axis)

def _gelu(x):
    return jax.nn.gelu(x, approximate=True)

def _silu(x):
    return jax.nn.silu(x)

def _sigmoid(x):
    return jax.nn.sigmoid(x)

def _layernorm(x, axis=-1, eps=1e-05):
    m = jnp.mean(x, axis=axis, keepdims=True)
    v = jnp.var(x, axis=axis, keepdims=True)
    return (x - m) / jnp.sqrt(v + eps)

def _scatter_add(tgt, idx, src, axis=0):
    return tgt.at[idx].add(src)

def _segment_sum(src, seg, n):
    return jax.ops.segment_sum(src, seg, n)
kernel_name = 'mk_rec_standalone_d1_rec_r8_8636de'

def setup_inputs(seed: int=0):
    np.random.seed(seed)
    _w = jnp.asarray

    def _rec_inputs():
        import jax
        import jax.numpy as jnp
        _rk = jax.random.key(seed)
        r_bottom_output = -0.000185639 + 0.999941 * jax.random.normal(jax.random.fold_in(_rk, 1), (2048, 27, 128), jnp.float32)
        return r_bottom_output
    r_bottom_output = _rec_inputs()

    def _L0_rec_setup():
        import jax, jax.numpy as jnp
        import numpy as np
        BATCH, NUM_INPUTS, EMB = (4096, 27, 128)
        TOP_SIZES = [1024, 1024, 512, 256, 1]
        INPUT_DIMS = NUM_INPUTS * (NUM_INPUTS - 1) // 2 + EMB + 1
        _TRIL_R, _TRIL_C = np.tril_indices(NUM_INPUTS, k=-1)
        key = jax.random.key(seed)
        ks = jax.random.split(key, 12)
        inp = {'bottom_output': jax.random.normal(ks[0], (BATCH, NUM_INPUTS, EMB), jnp.float32)}
        dims = [INPUT_DIMS] + TOP_SIZES
        for i in range(5):
            fan_in, fan_out = (dims[i], dims[i + 1])
            W = jax.random.normal(ks[1 + 2 * i], (fan_out, fan_in), jnp.float32) * np.sqrt(2.0 / (fan_in + fan_out))
            b = jax.random.normal(ks[2 + 2 * i], (fan_out,), jnp.float32) * np.sqrt(1.0 / fan_out)
            if i == 0:
                W = W.at[:, -1].set(0.0)
            inp[f'W{i}'] = W
            inp[f'b{i}'] = b
        return inp
    _L0_rec_all = _L0_rec_setup()
    _L0_rec_in = {k: v for k, v in _L0_rec_all.items() if k in ('W0', 'b0', 'W1', 'b1', 'W2', 'b2', 'W3', 'b3', 'W4', 'b4')}
    del _L0_rec_all
    return {'r_bottom_output': r_bottom_output, 'L0_rec_W0': _L0_rec_in['W0'], 'L0_rec_b0': _L0_rec_in['b0'], 'L0_rec_W1': _L0_rec_in['W1'], 'L0_rec_b1': _L0_rec_in['b1'], 'L0_rec_W2': _L0_rec_in['W2'], 'L0_rec_b2': _L0_rec_in['b2'], 'L0_rec_W3': _L0_rec_in['W3'], 'L0_rec_b3': _L0_rec_in['b3'], 'L0_rec_W4': _L0_rec_in['W4'], 'L0_rec_b4': _L0_rec_in['b4']}

def reference(r_bottom_output, L0_rec_W0, L0_rec_b0, L0_rec_W1, L0_rec_b1, L0_rec_W2, L0_rec_b2, L0_rec_W3, L0_rec_b3, L0_rec_W4, L0_rec_b4):
    import jax
    import jax.numpy as jnp

    def _L0_rec_ref(bottom_output, W0, b0, W1, b1, W2, b2, W3, b3, W4, b4):
        import jax, jax.numpy as jnp
        import numpy as np
        BATCH, NUM_INPUTS, EMB = (4096, 27, 128)
        TOP_SIZES = [1024, 1024, 512, 256, 1]
        INPUT_DIMS = NUM_INPUTS * (NUM_INPUTS - 1) // 2 + EMB + 1
        _TRIL_R, _TRIL_C = np.tril_indices(NUM_INPUTS, k=-1)
        b = bottom_output.shape[0]
        bottom_mlp_output = bottom_output[:, 0, :]
        interaction = jnp.einsum('bnd,bmd->bnm', bottom_output, bottom_output)
        interaction_flat = interaction[:, _TRIL_R, _TRIL_C]
        zero_pad = jnp.zeros((b, 1), bottom_output.dtype)
        x = jnp.concatenate([bottom_mlp_output, interaction_flat, zero_pad], axis=1)
        x = jax.nn.relu(x @ W0.T + b0)
        x = jax.nn.relu(x @ W1.T + b1)
        x = jax.nn.relu(x @ W2.T + b2)
        x = jax.nn.relu(x @ W3.T + b3)
        return x @ W4.T + b4
    y = _L0_rec_ref(r_bottom_output, L0_rec_W0, L0_rec_b0, L0_rec_W1, L0_rec_b1, L0_rec_W2, L0_rec_b2, L0_rec_W3, L0_rec_b3, L0_rec_W4, L0_rec_b4)
    return y

_drawn_inputs = setup_inputs


def setup_inputs(seed=0):
    import zlib

    import numpy as np

    out = dict(_drawn_inputs(seed))
    spreads = {}
    factors = {'L0_rec_b0': 8.0, 'L0_rec_b1': 8.0, 'L0_rec_b2': 4.431}
    for name, (base, spread) in spreads.items():
        noise = np.random.default_rng([zlib.crc32(name.encode()), seed]).standard_normal(out[name].shape)
        drawn = base * np.exp(spread * noise) if base else spread * noise
        out[name] = jnp.asarray(drawn.astype(out[name].dtype))
    for name, factor in factors.items():
        out[name] = (out[name] * factor).astype(out[name].dtype)
    return out
```

```python
import numpy as np
import concourse.bass as bass
from concourse import mybir
from contextlib import ExitStack

BATCH, INPUTS, EMB = 2048, 27, 128
SIZES = [1024, 1024, 512, 256]
P = 128
CHUNK = 512
CHUNKS = BATCH // CHUNK
SUB = 128
SUBS = CHUNK // SUB
GROUP = 4
QUAD = P // GROUP
GCOLS = GROUP * INPUTS
BANK_GROUPS = 4
BANK = 512
SLICE_GROUPS = 2 * BANK_GROUPS
SCOLS = SLICE_GROUPS * GCOLS
SLICES_SUB = SUB // (GROUP * SLICE_GROUPS)
SLICES = SUBS * SLICES_SUB
HALF = (INPUTS - 1) // 2
PAIR_TILES = 3
M_TILE = INPUTS // PAIR_TILES
PAIRS_TILE = M_TILE * HALF
KT0 = 1 + PAIR_TILES
ZERO_ROW = PAIRS_TILE
KT1, KT2, KT3 = SIZES[0] // P, SIZES[1] // P, SIZES[2] // P
MT0, MT1, MT2, MT3 = (s // P for s in SIZES)
TILES = MT0 + MT1 + MT2 + MT3
STAGE = 1024
W0_LOADS, W1_LOADS = KT0, MT1
W2_LOADS = KT2 * SIZES[2] // STAGE
W3_LOADS = 2
LOADS = W0_LOADS + W1_LOADS + W2_LOADS + W3_LOADS


def pair_features():
    rows = np.full((KT0, P), -1)
    rows[0] = np.arange(EMB)
    for t in range(PAIR_TILES):
        for i in range(PAIRS_TILE):
            m, k = M_TILE * t + i // HALF, 1 + i % HALF
            flat = (INPUTS + 1) * m + k
            if m == INPUTS - 1:
                r, c = k - 1, k + HALF
            else:
                r, c = flat // INPUTS, flat % INPUTS
            hi, lo = max(r, c), min(r, c)
            rows[1 + t, i] = EMB + hi * (hi - 1) // 2 + lo
    rows[KT0 - 1, ZERO_ROW] = EMB + INPUTS * (INPUTS - 1) // 2
    return rows


def rec_program(nc, x_t, x0_t, w0, w1, w2, w3, w4, biases, b4, out):
    f32, f32r = mybir.dt.float32, mybir.dt.float32r
    ALU = mybir.AluOpType
    ACT = mybir.ActivationFunctionType

    ctx = ExitStack()
    with ctx:
        def sb(name, shape, dt=f32):
            return ctx.enter_context(nc.sbuf_tensor(name, shape, dt))

        def sem(name):
            return ctx.enter_context(nc.semaphore(name))

        w0h, w0l = sb("w0h", [P, KT0, SIZES[0]], f32r), sb("w0l", [P, KT0, SIZES[0]], f32r)
        w1h = sb("w1h", [P, MT1, KT1 * P], f32r)
        w1l = sb("w1l", [P, 2, KT1 * P], f32r)
        w2h, w2l = sb("w2h", [P, KT2 * SIZES[2]], f32r), sb("w2l", [P, KT2 * SIZES[2]], f32r)
        w3h, w3l = sb("w3h", [P, KT3 * SIZES[3]], f32r), sb("w3l", [P, KT3 * SIZES[3]], f32r)
        w4raw = sb("w4raw", [P, MT3, 1])
        w4s = sb("w4s", [P, MT3, 2], f32r)
        stage = sb("stage", [P, 2, STAGE])
        bias = sb("bias", [P, MT0 + MT1 + MT2 + MT3])
        bias4 = sb("bias4", [P, 1])
        ident = sb("ident", [P, P])

        xraw = sb("xraw", [P, 2, SCOLS])
        xh = sb("xh", [P, 2, SLICE_GROUPS * GROUP, QUAD], f32r)
        xhh = sb("xhh", [P, 2, SCOLS], f32r)
        xl = sb("xl", [P, 2, SCOLS], f32r)
        x0raw = sb("x0raw", [P, CHUNK])
        grams = sb("grams", [P, SUB // GROUP, INPUTS])
        turned = sb("turned", [P, INPUTS, QUAD])
        sums = sb("sums", [P, INPUTS * INPUTS + HALF])
        pairs = sb("pairs", [P, PAIR_TILES * PAIRS_TILE])
        featH, featL = sb("featH", [P, KT0, CHUNK], f32r), sb("featL", [P, KT0, CHUNK], f32r)
        h1h, h1l = sb("h1h", [P, MT0, CHUNK], f32r), sb("h1l", [P, MT0, CHUNK], f32r)
        h2h, h2l = sb("h2h", [P, 2, CHUNK], f32r), sb("h2l", [P, 2, CHUNK], f32r)
        act_out = sb("act_out", [P, 2, CHUNK])
        ysum = sb("ysum", [P, SUBS])
        y = sb("y", [P, CHUNKS * SUBS])

        work = [ctx.enter_context(nc.psum_tensor(f"work{i}", [P, BANK], f32)) for i in range(2)]
        acc = [ctx.enter_context(nc.psum_tensor(f"acc{i}", [P, BANK], f32)) for i in range(4)]
        gps = ctx.enter_context(nc.psum_tensor("gps", [P, 2, BANK], f32))

        small_in = sem("small_in")
        w_in = [sem(f"w_in{i}") for i in range(2)]
        x_in = [sem(f"x_in{i}") for i in range(2)]
        x0_in = sem("x0_in")
        ident_zero, ident_done, pads_done, zero_done = sem("ident_zero"), sem("ident_done"), sem("pads_done"), sem("zero_done")
        w0_hi, w0_done = sem("w0_hi"), sem("w0_done")
        w_hi, w_done = sem("w_hi"), sem("w_done")
        w4_hi, w4_done = sem("w4_hi"), sem("w4_done")
        xh_done, xhh_done, xl_done = sem("xh_done"), sem("xhh_done"), sem("xl_done")
        gram_done, grams_out = sem("gram_done"), sem("grams_out")
        turned_done, sums_done, pairs_done = sem("turned_done"), sem("sums_done"), sem("pairs_done")
        pairs_t, pairs_hi, pairs_lo = sem("pairs_t"), sem("pairs_hi"), sem("pairs_lo")
        dense_hi, dense_done = sem("dense_hi"), sem("dense_done")
        tile_done, relu_done, hi_done, split_done = sem("tile_done"), sem("relu_done"), sem("hi_done"), sem("split_done")
        logits_done, ysum_done, y_done, out_done = sem("logits_done"), sem("ysum_done"), sem("y_done"), sem("out_done")

        def ge(eng, s, value):
            if not (isinstance(value, int) and value <= 0):
                eng.wait_ge(s, value)

        def by_sample(buf, p):
            return buf[:, p % 2, :].rearrange("p (b n) -> p b n", n=INPUTS)

        def weights_of(n):
            n -= W0_LOADS
            if n < W1_LOADS:
                return w1h[:, n, :], None, STAGE
            n -= W1_LOADS
            if n < W2_LOADS:
                return w2h[:, n * STAGE:(n + 1) * STAGE], w2l[:, n * STAGE:(n + 1) * STAGE], STAGE
            n -= W2_LOADS
            w = KT3 * SIZES[3] // W3_LOADS
            return w3h[:, n * w:(n + 1) * w], w3l[:, n * w:(n + 1) * w], w

        AFTER_L0 = {MT0 - 2: [0], MT0 - 1: [1]}
        AFTER_L1 = {m: [2 * m + 2, 2 * m + 3] for m in range(MT1 - 1)}

        block = ctx.enter_context(nc.Block())

        @block.sync
        def _(sp):
            def load_w(n, src, cols=STAGE):
                sp.dma_start(stage[:, n % 2, 0:cols], src).then_inc(w_in[n % 2], 16)

            def load_x(g, p):
                n = SLICES * g + p
                ge(sp, xl_done, n - 1)
                ge(sp, xhh_done, n - 1)
                sp.dma_start(xraw[:, p % 2, :], x_t[n, :, :]).then_inc(x_in[p % 2], 16)

            def load_x0(g):
                ge(sp, dense_done, g)
                sp.dma_start(x0raw[:, :], x0_t[g, :, :]).then_inc(x0_in, 16)

            def load_w1(c, m):
                sp.wait_ge(w_done, LOADS - W0_LOADS + MT1 * c + m - 1)
                sp.dma_start(stage[:, m % 2, :], w1[m, :, :]).then_inc(w_in[m % 2], 16)

            sp.dma_start(bias[:, :], biases).then_inc(small_in, 16)
            sp.dma_start(bias4[:, :], b4.to_broadcast([P, 1])).then_inc(small_in, 16)
            sp.dma_start(w4raw[:, :, :], w4).then_inc(small_in, 16)
            for n in range(W0_LOADS):
                ge(sp, w0_done, n - 1)
                load_w(n, w0[n, :, :])
            load_x0(0)
            for p in range(SLICES):
                load_x(0, p)
            for n in range(W0_LOADS, LOADS):
                if n - 2 < W0_LOADS:
                    sp.wait_ge(w0_done, n - 1)
                else:
                    sp.wait_ge(w_done, n - 1 - W0_LOADS)
                i = n - W0_LOADS
                if i < W1_LOADS:
                    load_w(n, w1[i, :, :])
                elif i < W1_LOADS + W2_LOADS:
                    load_w(n, w2[i - W1_LOADS, :, :])
                else:
                    load_w(n, w3[i - W1_LOADS - W2_LOADS, :, :], KT3 * SIZES[3] // W3_LOADS)

            def body(c, more):
                if more:
                    load_x0(c + 1)
                    load_x(c + 1, 0)
                    load_x(c + 1, 1)
                load_w1(c, 0)
                load_w1(c, 1)
                for m in range(MT1):
                    if more:
                        for p in AFTER_L1.get(m, []):
                            load_x(c + 1, p)
                    if m + 2 < MT1:
                        load_w1(c, m + 2)

            with sp.Fori(0, CHUNKS - 1) as c:
                body(c, True)
            body(CHUNKS - 1, False)
            sp.wait_ge(y_done, CHUNKS)
            sp.dma_start(out, y[:, :]).then_inc(out_done, 16)
            sp.wait_ge(out_done, 16)

        @block.gpsimd
        def _(pool):
            pool.memset(ident[:, :], 0.0).then_inc(ident_zero, 1)
            pool.wait_ge(ident_zero, 1)
            pool.affine_select(out=ident[:, :], in_=ident[:, :], compare_op=ALU.not_equal, fill=1.0, base=0,
                               pattern=[[-1, P]], channel_multiplier=1).then_inc(ident_done, 1)

            def input_lo(g, p):
                n = SLICES * g + p
                pool.wait_ge(xh_done, n + 1)
                ge(pool, gram_done, n - 1)
                pool.tensor_tensor(by_sample(xl, p), by_sample(xraw, p), xh[:, p % 2, :, 0:INPUTS].bitcast(f32),
                                   ALU.subtract).then_inc(xl_done, 1)

            def w1_lo(c, m):
                n = LOADS + m
                pool.wait_ge(w_in[m % 2], 16 * (MT1 // 2 * c + n // 2 + 1))
                if m >= 2:
                    pool.wait_ge(tile_done, TILES * c + MT0 + m - 1)
                else:
                    pool.wait_ge(tile_done, TILES * c + 1)
                pool.tensor_tensor(w1l[:, m % 2, :], stage[:, m % 2, :], w1h[:, m, :].bitcast(f32),
                                   ALU.subtract).then_inc(w_done, 1)

            for p in range(SLICES):
                input_lo(0, p)
            for n in range(W0_LOADS, LOADS):
                hi, lo, cols = weights_of(n)
                pool.wait_ge(w_in[n % 2], 16 * (n // 2 + 1))
                done = n - W0_LOADS
                if lo is None:
                    pool.tensor_copy(hi, stage[:, n % 2, 0:cols]).then_inc(w_done, 1)
                else:
                    pool.tensor_copy(hi, stage[:, n % 2, 0:cols]).then_inc(w_hi, 1)
                    pool.wait_ge(w_hi, done - W1_LOADS + 1)
                    pool.tensor_tensor(lo, stage[:, n % 2, 0:cols], hi.bitcast(f32), ALU.subtract).then_inc(w_done, 1)
            pool.wait_ge(w_done, LOADS - W0_LOADS)

            def body(c, more):
                if more:
                    input_lo(c + 1, 0)
                    input_lo(c + 1, 1)
                w1_lo(c, 0)
                w1_lo(c, 1)
                for m in range(MT1):
                    if more:
                        for p in AFTER_L1.get(m, []):
                            input_lo(c + 1, p)
                    if m + 2 < MT1:
                        w1_lo(c, m + 2)

            with pool.Fori(0, CHUNKS - 1) as c:
                body(c, True)
            body(CHUNKS - 1, False)

        @block.scalar
        def _(act):
            def half_hi(g, p):
                n = SLICES * g + p
                act.wait_ge(x_in[p % 2], 16 * (SLICES // 2 * g + p // 2 + 1))
                ge(act, gram_done, n - 1)
                act.activation(xhh[:, p % 2, :], xraw[:, p % 2, :], ACT.Copy, scale=0.5).then_inc(xhh_done, 1)

            def grams_from_psum(g, p):
                n = SLICES * g + p
                act.wait_ge(gram_done, n + 1)
                if p % SLICES_SUB == 0:
                    ge(act, turned_done, SUBS * g + p // SLICES_SUB)
                first = p % SLICES_SUB * SLICE_GROUPS
                for q in range(GROUP):
                    rows = slice(q * QUAD, (q + 1) * QUAD)
                    src = gps[rows, :, 0:BANK_GROUPS * GCOLS].rearrange("p b (g c) -> p b g c", c=GCOLS)
                    dst = grams[rows, first:first + SLICE_GROUPS, :].rearrange("p (b g) c -> p b g c", b=2)
                    last = act.activation(dst, src[:, :, :, q * INPUTS:(q + 1) * INPUTS], ACT.Copy)
                last.then_inc(grams_out, 1)

            def slice_point(g, p):
                if p + 1 < SLICES:
                    half_hi(g, p + 1)
                grams_from_psum(g, p)

            def pairs_hi_part(g, s):
                act.wait_ge(pairs_t, SUBS * g + s + 1)
                dst = featH[0:PAIRS_TILE, 1:KT0, s * SUB:(s + 1) * SUB]
                src = gps[0:PAIRS_TILE, 0, 0:PAIR_TILES * SUB].rearrange("p (t b) -> p t b", b=SUB)
                act.activation(dst, src, ACT.Copy).then_inc(pairs_hi, 1)

            def relu(c, i, bank):
                n = TILES * c + i
                act.wait_ge(tile_done, n + 1)
                if i >= 2:
                    act.wait_ge(split_done, n - 1)
                act.activation(act_out[:, i % 2, :], bank[:, :], ACT.Relu, bias=bias[:, i:i + 1]).then_inc(relu_done, 1)

            half_hi(0, 0)
            for p in range(SLICES):
                slice_point(0, p)
                if p % SLICES_SUB == 0 and p:
                    pairs_hi_part(0, p // SLICES_SUB - 1)
            pairs_hi_part(0, SUBS - 1)
            act.wait_ge(small_in, 48)

            def body(c, more):
                for m in range(MT0):
                    if more and m == MT0 - 2:
                        half_hi(c + 1, 0)
                    relu(c, m, work[m % 2])
                    if more:
                        for p in AFTER_L0.get(m, []):
                            slice_point(c + 1, p)
                for m in range(MT1):
                    here = list(AFTER_L1.get(m, [])) if more else []
                    if more and m % 2:
                        pairs_hi_part(c + 1, m // 2)
                    if m == 0 and here:
                        slice_point(c + 1, here.pop(0))
                    relu(c, MT0 + m, work[m % 2])
                    for p in here:
                        slice_point(c + 1, p)
                for m in range(MT2):
                    relu(c, MT0 + MT1 + m, acc[m])
                for m in range(MT3):
                    relu(c, MT0 + MT1 + MT2 + m, acc[m])

            with act.Fori(0, CHUNKS - 1) as c:
                body(c, True)
            body(CHUNKS - 1, False)

        @block.vector
        def _(dve):
            dve.memset(xh[:, :, :, :].bitcast(f32), 0.0).then_inc(pads_done, 1)
            dve.memset(featH[:, :, :].bitcast(f32), 0.0).then_inc(zero_done, 1)
            dve.memset(featL[:, :, :].bitcast(f32), 0.0).then_inc(zero_done, 1)

            def input_hi(g, p):
                n = SLICES * g + p
                dve.wait_ge(x_in[p % 2], 16 * (SLICES // 2 * g + p // 2 + 1))
                ge(dve, gram_done, n - 1)
                dve.tensor_copy(xh[:, p % 2, :, 0:INPUTS], by_sample(xraw, p)).then_inc(xh_done, 1)

            def dense_parts(g):
                dve.wait_ge(x0_in, 16 * (g + 1))
                dve.tensor_copy(featH[:, 0, :], x0raw[:, :]).then_inc(dense_hi, 1)
                dve.wait_ge(dense_hi, g + 1)
                dve.tensor_tensor(featL[:, 0, :], x0raw[:, :], featH[:, 0, :].bitcast(f32), ALU.subtract)\
                   .then_inc(dense_done, 1)

            def pair_products(g, s):
                n = SUBS * g + s
                dve.wait_ge(grams_out, SLICES_SUB * (n + 1))
                ge(dve, sums_done, 2 * n)
                dve.transpose(turned[:, :, :], grams[:, :, :].rearrange("p g m -> p m g")).then_inc(turned_done, 1)
                dve.wait_ge(turned_done, n + 1)
                ge(dve, pairs_done, n)
                full = turned[:, :, 0:INPUTS]
                dve.tensor_tensor(sums[:, 0:INPUTS * INPUTS].rearrange("p (i j) -> p i j", j=INPUTS),
                                  full, full.rearrange("p i j -> p j i"), ALU.add).then_inc(sums_done, 1)
                v = turned[:, 0, 0:HALF]
                above = bass.AP(v.tensor, v.offset + HALF + 1, [v.ap[0], (QUAD + 1, HALF)])
                below = bass.AP(v.tensor, v.offset + QUAD * (HALF + 1), [v.ap[0], (QUAD + 1, HALF)])
                dve.tensor_tensor(sums[:, INPUTS * INPUTS:], above, below, ALU.add).then_inc(sums_done, 1)
                dve.wait_ge(sums_done, 2 * (n + 1))
                ge(dve, pairs_t, n)
                v = sums[:, 1:1 + HALF]
                once = bass.AP(v.tensor, v.offset, [v.ap[0], (INPUTS + 1, INPUTS), (1, HALF)])
                dve.tensor_copy(pairs[:, :].rearrange("p (m k) -> p m k", k=HALF), once).then_inc(pairs_done, 1)

            def slice_point(g, p):
                if p + 1 < SLICES:
                    input_hi(g, p + 1)
                if p % SLICES_SUB == SLICES_SUB - 1:
                    pair_products(g, p // SLICES_SUB)

            def pairs_lo_part(g, s):
                dve.wait_ge(pairs_hi, SUBS * g + s + 1)
                at = slice(s * SUB, (s + 1) * SUB)
                src = gps[0:PAIRS_TILE, 0, 0:PAIR_TILES * SUB].rearrange("p (t b) -> p t b", b=SUB)
                dve.tensor_tensor(featL[0:PAIRS_TILE, 1:KT0, at], src, featH[0:PAIRS_TILE, 1:KT0, at].bitcast(f32),
                                  ALU.subtract).then_inc(pairs_lo, 1)

            def split(c, i, hi, lo):
                n = TILES * c + i
                dve.wait_ge(relu_done, n + 1)
                dve.tensor_copy(hi, act_out[:, i % 2, :]).then_inc(hi_done, 1)
                dve.wait_ge(hi_done, n + 1)
                dve.tensor_tensor(lo, act_out[:, i % 2, :], hi.bitcast(f32), ALU.subtract).then_inc(split_done, 1)

            for n in range(W0_LOADS):
                dve.wait_ge(w_in[n % 2], 16 * (n // 2 + 1))
                dve.tensor_copy(w0h[:, n, :], stage[:, n % 2, :]).then_inc(w0_hi, 1)
                dve.wait_ge(w0_hi, n + 1)
                dve.tensor_tensor(w0l[:, n, :], stage[:, n % 2, :], w0h[:, n, :].bitcast(f32), ALU.subtract)\
                   .then_inc(w0_done, 1)
            dve.wait_ge(small_in, 48)
            dve.tensor_copy(w4s[:, :, 0:1], w4raw[:, :, :]).then_inc(w4_hi, 1)
            dve.wait_ge(w4_hi, 1)
            dve.tensor_tensor(w4s[:, :, 1:2], w4raw[:, :, :], w4s[:, :, 0:1].bitcast(f32), ALU.subtract)\
               .then_inc(w4_done, 1)
            dve.wait_ge(zero_done, 2)
            dense_parts(0)
            input_hi(0, 0)
            for p in range(SLICES):
                slice_point(0, p)
                if p % SLICES_SUB == 0 and p:
                    pairs_lo_part(0, p // SLICES_SUB - 1)
            pairs_lo_part(0, SUBS - 1)

            def body(c, more):
                for m in range(MT0):
                    if more and m == MT0 - 2:
                        input_hi(c + 1, 0)
                    split(c, m, h1h[:, m, :], h1l[:, m, :])
                    if more:
                        for p in AFTER_L0.get(m, []):
                            slice_point(c + 1, p)
                for m in range(MT1):
                    here = list(AFTER_L1.get(m, [])) if more else []
                    if more and m % 2:
                        pairs_lo_part(c + 1, m // 2)
                    if m == 0 and here:
                        slice_point(c + 1, here.pop(0))
                    split(c, MT0 + m, h2h[:, m % 2, :], h2l[:, m % 2, :])
                    if more and m == 0:
                        dense_parts(c + 1)
                    for p in here:
                        slice_point(c + 1, p)
                for m in range(MT2):
                    split(c, MT0 + MT1 + m, h1h[:, m, :], h1l[:, m, :])
                for m in range(MT3):
                    split(c, MT0 + MT1 + MT2 + m, h2h[:, m, :], h2l[:, m, :])
                dve.wait_ge(logits_done, c + 1)
                dve.tensor_reduce(ysum[:, :], acc[3][:, 0:2 * SUBS].rearrange("p (s t) -> p s t", t=2),
                                  mybir.AxisListType.X, ALU.add).then_inc(ysum_done, 1)
                dve.wait_ge(ysum_done, c + 1)
                at = slice(c * SUBS, (c + 1) * SUBS) if isinstance(c, int) else bass.ts(c, SUBS)
                dve.tensor_scalar(y[:, at], ysum[:, :], bias4[:, 0:1], None, ALU.add).then_inc(y_done, 1)

            with dve.Fori(0, CHUNKS - 1) as c:
                body(c, True)
            body(CHUNKS - 1, False)

        @block.tensor
        def _(pe):
            def product(dst, wh, wl, ah, al, start, stop):
                pe.matmul(dst, wl, ah, start=start, stop=False)
                pe.matmul(dst, wh, ah, start=False, stop=False)
                return pe.matmul(dst, wh, al, start=False, stop=stop)

            def gram_slice(g, p, before):
                n = SLICES * g + p
                pe.wait_ge(xh_done, n + 1)
                pe.wait_ge(xhh_done, n + 1)
                pe.wait_ge(xl_done, n + 1)
                ge(pe, grams_out, n)
                ge(pe, pairs_lo, SUBS * g + before)
                for k in range(SLICE_GROUPS):
                    four = xh[:, p % 2, k * GROUP:(k + 1) * GROUP, :].rearrange("p b n -> p (b n)")
                    b, at = k // BANK_GROUPS, k % BANK_GROUPS * GCOLS
                    dst = gps[:, b, at:at + GCOLS]
                    pe.matmul(dst, four, xhh[:, p % 2, k * GCOLS:(k + 1) * GCOLS], start=True, stop=False)
                    last = pe.matmul(dst, four, xl[:, p % 2, k * GCOLS:(k + 1) * GCOLS], start=False, stop=True)
                last.then_inc(gram_done, 1)

            def transpose_pairs(g, s, before):
                n = SUBS * g + s
                pe.wait_ge(pairs_done, n + 1)
                ge(pe, grams_out, SLICES * g + before)
                for t in range(PAIR_TILES):
                    last = pe.transpose(gps[0:PAIRS_TILE, 0, t * SUB:(t + 1) * SUB],
                                        pairs[:, t * PAIRS_TILE:(t + 1) * PAIRS_TILE], ident[:, :])
                last.then_inc(pairs_t, 1)

            def layer0(c, m):
                if m == 0:
                    pe.wait_ge(dense_done, c + 1)
                    pe.wait_ge(pairs_lo, SUBS * (c + 1))
                if m >= 2:
                    pe.wait_ge(relu_done, TILES * c + m - 1)
                cols = slice(m * P, (m + 1) * P)
                for k in range(KT0):
                    rows = slice(0, P if k == 0 else PAIRS_TILE if k < KT0 - 1 else ZERO_ROW + 1)
                    last = product(work[m % 2][:, :], w0h[rows, k, cols], w0l[rows, k, cols],
                                   featH[rows, k, :], featL[rows, k, :], k == 0, k == KT0 - 1)
                last.then_inc(tile_done, 1)

            def layer1(c, m, ks):
                if ks[0] == 0:
                    pe.wait_ge(w_done, LOADS - W0_LOADS + MT1 * c + m + 1)
                    ge(pe, relu_done, TILES * c + MT0 + m - 1)
                for k in ks:
                    if m == 0:
                        pe.wait_ge(split_done, TILES * c + k + 1)
                    cols = slice(k * P, (k + 1) * P)
                    last = product(work[m % 2][:, :], w1h[:, m, cols], w1l[:, m % 2, cols],
                                   h1h[:, k, :], h1l[:, k, :], k == 0, k == KT1 - 1)
                if ks[-1] == KT1 - 1:
                    last.then_inc(tile_done, 1)

            def layer2(c, k):
                pe.wait_ge(split_done, TILES * c + MT0 + k + 1)
                for m in range(MT2):
                    cols = slice(k * SIZES[2] + m * P, k * SIZES[2] + (m + 1) * P)
                    last = product(acc[m][:, :], w2h[:, cols], w2l[:, cols], h2h[:, k % 2, :], h2l[:, k % 2, :],
                                   k == 0, k == KT2 - 1)
                    if k == KT2 - 1:
                        last.then_inc(tile_done, 1)

            def layer3(c, m):
                for k in range(KT3):
                    if m == 0:
                        pe.wait_ge(split_done, TILES * c + MT0 + MT1 + k + 1)
                    cols = slice(k * SIZES[3] + m * P, k * SIZES[3] + (m + 1) * P)
                    last = product(acc[m][:, :], w3h[:, cols], w3l[:, cols], h1h[:, k, :], h1l[:, k, :],
                                   k == 0, k == KT3 - 1)
                last.then_inc(tile_done, 1)

            def layer4(c):
                for k in range(MT3):
                    pe.wait_ge(split_done, TILES * c + TILES - MT3 + k + 1)
                for s in range(SUBS):
                    for k in range(MT3):
                        at = slice(s * SUB, (s + 1) * SUB)
                        dst = acc[3][:, 2 * s:2 * s + 2]
                        pe.matmul(dst, h2h[:, k, at], w4s[:, k, :], start=k == 0, stop=False)
                        last = pe.matmul(dst, h2l[:, k, at], w4s[:, k, :], start=False, stop=k == MT3 - 1)
                last.then_inc(logits_done, 1)

            pe.wait_ge(pads_done, 1)
            pe.wait_ge(ident_done, 1)
            for p in range(SLICES):
                gram_slice(0, p, max(p - 1, 0) // SLICES_SUB)
                if p % SLICES_SUB == 0 and p:
                    transpose_pairs(0, p // SLICES_SUB - 1, p + 1)
            transpose_pairs(0, SUBS - 1, SLICES)
            pe.wait_ge(w0_done, W0_LOADS)
            pe.wait_ge(w4_done, 1)

            def body(c, more):
                for m in range(MT0):
                    layer0(c, m)
                    if more:
                        for p in AFTER_L0.get(m, []):
                            gram_slice(c + 1, p, 0)
                pe.wait_ge(w_done, W1_LOADS)
                for m in range(MT1):
                    here = list(AFTER_L1.get(m, [])) if more else []
                    if m == 1:
                        pe.wait_ge(w_done, W1_LOADS + W2_LOADS)
                    layer1(c, m, range(0, KT1 // 2))
                    if more and m % 2:
                        transpose_pairs(c + 1, m // 2, SLICES_SUB * (m // 2 + 1))
                    if m == 0 and here:
                        gram_slice(c + 1, here.pop(0), (m + 1) // 2)
                    layer1(c, m, range(KT1 // 2, KT1))
                    if here:
                        gram_slice(c + 1, here.pop(0), (m + 1) // 2)
                    if m:
                        layer2(c, m - 1)
                    if here:
                        gram_slice(c + 1, here.pop(0), (m + 1) // 2)
                layer2(c, KT2 - 1)
                pe.wait_ge(w_done, LOADS - W0_LOADS)
                for m in range(MT3):
                    layer3(c, m)
                layer4(c)
    
            with pe.Fori(0, CHUNKS - 1) as c:
                body(c, True)
            body(CHUNKS - 1, False)


def kernel(**inputs):
    import concourse.bacc as _bacc
    from concourse.bass_utils import run_bass_kernel_spmd as _run

    x = np.ascontiguousarray(inputs["r_bottom_output"])
    W = [np.ascontiguousarray(inputs[f"L0_rec_W{i}"]) for i in range(5)]
    b = [np.ascontiguousarray(inputs[f"L0_rec_b{i}"]) for i in range(5)]

    xs = x.reshape(GROUP, QUAD, CHUNKS * SUBS, INPUTS, EMB)
    x_t = xs.transpose(2, 1, 0, 3, 4).reshape(CHUNKS * SLICES, SLICE_GROUPS * GROUP * INPUTS, EMB).transpose(0, 2, 1)
    x0_t = x[:, 0, :].reshape(P, CHUNKS, SUBS, EMB).transpose(1, 3, 2, 0).reshape(CHUNKS, EMB, CHUNK)

    rows = pair_features()
    w0 = np.zeros((KT0, P, SIZES[0]), W[0].dtype)
    w0[rows >= 0] = W[0].T[rows[rows >= 0]]
    w1 = W[1].reshape(MT1, P, KT1, P).transpose(0, 3, 2, 1).reshape(MT1, P, KT1 * P)
    w2 = W[2].T.reshape(KT2, P, SIZES[2]).transpose(1, 0, 2).reshape(P, W2_LOADS, STAGE).transpose(1, 0, 2)
    w3 = W[3].T.reshape(KT3, P, SIZES[3]).transpose(1, 0, 2).reshape(P, W3_LOADS, KT3 * SIZES[3] // W3_LOADS).transpose(1, 0, 2)
    w4 = W[4].reshape(MT3, P, 1).transpose(1, 0, 2)
    biases = np.concatenate([v.reshape(-1, P) for v in b[:4]]).T

    nc = _bacc.Bacc("TRN2", target_bir_lowering=False, num_devices=1, dynamic_dma_scratch_size=1024)
    arrays = {}

    def given(name, a):
        arrays[name] = np.ascontiguousarray(a)
        return nc.dram_tensor(name, arrays[name].shape, mybir.dt.from_np(a.dtype), kind="ExternalInput").ap()

    args = [given("x_t", x_t), given("x0_t", x0_t), given("w0_t", w0), given("w1_t", w1), given("w2_t", w2),
            given("w3_t", w3), given("w4_t", w4), given("biases", biases), given("b4", b[4].reshape(1, 1))]
    out = nc.dram_tensor("out_0", (BATCH, 1), mybir.dt.float32, kind="ExternalOutput").ap()
    rec_program(nc, *args, out.rearrange("(p t) a -> p (t a)", p=P))
    r = _run(nc, [arrays], core_ids=[0])
    return r.results[0]["out_0"]
```

```python
import numpy as np
import concourse.bass as bass
from concourse import mybir
from contextlib import ExitStack

BATCH, INPUTS, EMB = 2048, 27, 128
SIZES = [1024, 1024, 512, 256]
P = 128
CHUNK = 512
CHUNKS = BATCH // CHUNK
SUB = 128
SUBS = CHUNK // SUB
GROUP = 4
QUAD = P // GROUP
SLICE_GROUPS = 8
HALF_GROUPS = SLICE_GROUPS // 2
SCOLS = SLICE_GROUPS * GROUP * INPUTS
BANK = 512
SLICES_SUB = SUB // (GROUP * SLICE_GROUPS)
SLICES = SUBS * SLICES_SUB
HALVES = 2 * SLICES
APART = (INPUTS - 1) // 2
PAIR_TILES = 3
M_TILE = INPUTS // PAIR_TILES
PAIRS_TILE = M_TILE * APART
KT0 = 1 + PAIR_TILES
ZERO_ROW = PAIRS_TILE
XSLOTS = 4
KT1, KT2, KT3 = SIZES[0] // P, SIZES[1] // P, SIZES[2] // P
MT0, MT1, MT2, MT3 = (s // P for s in SIZES)
TILES = MT0 + MT1 + MT2 + MT3
STAGE = 1024
W0_LOADS = KT0
W2_LOADS = KT2 * SIZES[2] // STAGE
W3_LOADS = 2
LOADS = W0_LOADS + W2_LOADS + W3_LOADS
assert LOADS % 2 == 0 and MT1 % 2 == 0 and SLICES % XSLOTS == 0


def pair_features():
    rows = np.full((KT0, P), -1)
    rows[0] = np.arange(EMB)
    for t in range(PAIR_TILES):
        for i in range(PAIRS_TILE):
            m, k = M_TILE * t + i // APART, 1 + i % APART
            flat = (INPUTS + 1) * m + k
            if m == INPUTS - 1:
                r, c = k - 1, k + APART
            else:
                r, c = flat // INPUTS, flat % INPUTS
            hi, lo = max(r, c), min(r, c)
            rows[1 + t, i] = EMB + hi * (hi - 1) // 2 + lo
    rows[KT0 - 1, ZERO_ROW] = EMB + INPUTS * (INPUTS - 1) // 2
    return rows


def rec_program(nc, x_t, x0_t, w0, w1, w2, w3, w4, biases, b4, out):
    f32, f32r = mybir.dt.float32, mybir.dt.float32r
    ALU = mybir.AluOpType
    ACT = mybir.ActivationFunctionType

    ctx = ExitStack()
    with ctx:
        def sb(name, shape, dt=f32):
            return ctx.enter_context(nc.sbuf_tensor(name, shape, dt))

        def sem(name):
            return ctx.enter_context(nc.semaphore(name))

        w0h, w0l = sb("w0h", [P, KT0, SIZES[0]], f32r), sb("w0l", [P, KT0, SIZES[0]], f32r)
        w1h, w1l = sb("w1h", [P, 2, KT1 * P], f32r), sb("w1l", [P, 2, KT1 * P], f32r)
        w2h, w2l = sb("w2h", [P, KT2 * SIZES[2]], f32r), sb("w2l", [P, KT2 * SIZES[2]], f32r)
        w3h, w3l = sb("w3h", [P, KT3 * SIZES[3]], f32r), sb("w3l", [P, KT3 * SIZES[3]], f32r)
        w4raw = sb("w4raw", [P, MT3, 1])
        w4s = sb("w4s", [P, MT3, 2], f32r)
        stage = sb("stage", [P, 2, STAGE])
        bias = sb("bias", [P, MT0 + MT1 + MT2 + MT3])
        bias4 = sb("bias4", [P, 1])
        ident = sb("ident", [P, P])

        xraw = sb("xraw", [P, XSLOTS, SCOLS])
        xs = sb("xs", [P, XSLOTS, 2, SLICE_GROUPS * GROUP, QUAD], f32r)
        x0raw = sb("x0raw", [P, CHUNK])
        grams2 = sb("grams2", [P, 2, SLICE_GROUPS, 2, INPUTS])
        grams = sb("grams", [P, SUB // GROUP, INPUTS])
        turned = sb("turned", [P, INPUTS, QUAD])
        sums = sb("sums", [P, INPUTS * INPUTS + APART])
        pairs = sb("pairs", [P, PAIR_TILES * PAIRS_TILE])
        featH, featL = sb("featH", [P, KT0, CHUNK], f32r), sb("featL", [P, KT0, CHUNK], f32r)
        h1h, h1l = sb("h1h", [P, MT0, CHUNK], f32r), sb("h1l", [P, MT0, CHUNK], f32r)
        h2h, h2l = sb("h2h", [P, 2, CHUNK], f32r), sb("h2l", [P, 2, CHUNK], f32r)
        act_out = sb("act_out", [P, 2, CHUNK])
        ysum = sb("ysum", [P, SUBS])
        y = sb("y", [P, CHUNKS * SUBS])
        H3 = MT0 - MT2

        work = ctx.enter_context(nc.psum_tensor("work", [P, 2, BANK], f32))
        acc = ctx.enter_context(nc.psum_tensor("acc", [P, 4, BANK], f32))
        gps = ctx.enter_context(nc.psum_tensor("gps", [P, 2, BANK], f32))

        small_in = sem("small_in")
        w_in = [sem(f"w_in{i}") for i in range(2)]
        x_in = [sem(f"x_in{i}") for i in range(XSLOTS)]
        x0_in = sem("x0_in")
        ident_zero, ident_done, pads_done, zero_done = sem("ident_zero"), sem("ident_done"), sem("pads_done"), sem("zero_done")
        w0_hi, w0_done = sem("w0_hi"), sem("w0_done")
        w_hi, w_done = sem("w_hi"), sem("w_done")
        w4_hi, w4_done = sem("w4_hi"), sem("w4_done")
        xh_done, xl_done = sem("xh_done"), sem("xl_done")
        gram_done, grams_out, half_sums = sem("gram_done"), sem("grams_out"), sem("half_sums")
        turned_done, sums_done, pairs_done = sem("turned_done"), sem("sums_done"), sem("pairs_done")
        pairs_t, pairs_hi, pairs_lo = sem("pairs_t"), sem("pairs_hi"), sem("pairs_lo")
        dense_hi, dense_done = sem("dense_hi"), sem("dense_done")
        tile_done, relu_done, hi_done, split_done = sem("tile_done"), sem("relu_done"), sem("hi_done"), sem("split_done")
        logits_done, ysum_done, y_done, out_done = sem("logits_done"), sem("ysum_done"), sem("y_done"), sem("out_done")

        def ge(eng, s, value):
            if not (isinstance(value, int) and value <= 0):
                eng.wait_ge(s, value)

        def by_sample(buf, p):
            return buf[:, p % XSLOTS, :].rearrange("p (b n) -> p b n", n=INPUTS)

        REST = LOADS - W0_LOADS

        def w23_parts(n):
            if n < W2_LOADS:
                return w2h[:, n * STAGE:(n + 1) * STAGE], w2l[:, n * STAGE:(n + 1) * STAGE], STAGE
            w, n = KT3 * SIZES[3] // W3_LOADS, n - W2_LOADS
            return w3h[:, n * w:(n + 1) * w], w3l[:, n * w:(n + 1) * w], w

        def staged(c, m):
            return 16 * (MT1 // 2 * c + (LOADS + m) // 2 + 1)

        EARLY = 2

        def nth(c, layer, m, more=True):
            if layer == 0 and m < EARLY:
                return m if isinstance(c, int) and c == 0 else TILES * c + (m - EARLY if m == 0 else m)
            first = {0: 0, 1: MT0, 2: MT0 + MT1, 3: MT0 + MT1 + MT2 + (1 if more else 0)}
            return TILES * c + first[layer] + m

        def slot(layer, m, more=True):
            return nth(0, layer, m, more) % 2 if (layer, m) != (0, 1) else 1

        FIRST_HALF = MT0 // 2
        AT_K = [0, 2, 6, KT1]
        IN_L1 = {(m, k): 4 * m + 4 + j for m in range(1, MT1 - 1) for j, k in enumerate(AT_K)}
        IN_L1.update({(0, k): 4 + j for j, k in enumerate([0, 2, 4, 6])})
        TURN_AT_K = 4

        def ahead(m):
            return range(2 * m + XSLOTS + 1, min(2 * m + XSLOTS + 3, SLICES))

        def gram_banks(first, h):
            return acc[:, 0:2, :] if first and h % 2 else gps[:, :, :]

        def pair_bank(first):
            return acc[:, 2, :] if first else gps[:, 0, :]

        block = ctx.enter_context(nc.Block())

        def interleave(on_half, on_turn, on_tile):
            for m in range(EARLY, MT0):
                on_tile(0, m)
                if m >= FIRST_HALF:
                    on_half(m - FIRST_HALF)
            for m in range(MT1):
                for k in range(KT1 + 1):
                    if (m, k) in IN_L1:
                        on_half(IN_L1[m, k])
                    if m % 2 and k == TURN_AT_K:
                        on_turn(m // 2)
                    if k == KT1 - 1:
                        on_tile(1, m)

        @block.sync
        def _(sp):
            def load_x(g, p):
                n = SLICES * g + p
                ge(sp, xl_done, n - XSLOTS + 1)
                sp.dma_start(xraw[:, p % XSLOTS, :], x_t[n, :, :]).then_inc(x_in[p % XSLOTS], 16)

            def load_x0(g):
                ge(sp, dense_done, g)
                sp.dma_start(x0raw[:, :], x0_t[g, :, :]).then_inc(x0_in, 16)

            def load_w1(c, m):
                sp.wait_ge(w_done, REST + MT1 * c + m - 1)
                sp.dma_start(stage[:, m % 2, :], w1[m, :, :]).then_inc(w_in[m % 2], 16)

            sp.dma_start(bias[:, :], biases).then_inc(small_in, 16)
            sp.dma_start(bias4[:, :], b4.to_broadcast([P, 1])).then_inc(small_in, 16)
            sp.dma_start(w4raw[:, :, :], w4).then_inc(small_in, 16)
            for p in range(SLICES):
                load_x(0, p)
                if p == 1:
                    load_x0(0)
                if p % 4 == 1:
                    n = p // 4
                    ge(sp, w0_done, n - 1)
                    sp.dma_start(stage[:, n % 2, :], w0[n, :, :]).then_inc(w_in[n % 2], 16)
            for n in range(REST):
                ge(sp, w0_done, min(n + 3, W0_LOADS))
                ge(sp, w_done, n - 1)
                src = w2[n, :, :] if n < W2_LOADS else w3[n - W2_LOADS, :, :]
                sp.dma_start(stage[:, n % 2, 0:src.shape[1]], src).then_inc(w_in[n % 2], 16)

            def body(c, more):
                if more:
                    load_x0(c + 1)
                    for p in range(XSLOTS):
                        load_x(c + 1, p)
                load_w1(c, 0)
                load_w1(c, 1)
                if more:
                    load_x(c + 1, XSLOTS)
                for m in range(MT1):
                    for p in ahead(m) if more else []:
                        load_x(c + 1, p)
                    if m + 2 < MT1:
                        load_w1(c, m + 2)

            with sp.Fori(0, CHUNKS - 1) as c:
                body(c, True)
            body(CHUNKS - 1, False)
            sp.wait_ge(y_done, CHUNKS)
            sp.dma_start(out, y[:, :]).then_inc(out_done, 16)
            sp.wait_ge(out_done, 16)

        @block.gpsimd
        def _(pool):
            pool.memset(ident[:, :], 0.0).then_inc(ident_zero, 1)
            pool.wait_ge(ident_zero, 1)
            pool.affine_select(out=ident[:, :], in_=ident[:, :], compare_op=ALU.not_equal, fill=1.0, base=0,
                               pattern=[[-1, P]], channel_multiplier=1).then_inc(ident_done, 1)

            def input_lo(g, p):
                n = SLICES * g + p
                pool.wait_ge(xh_done, n + 1)
                ge(pool, gram_done, 2 * (n - XSLOTS + 1))
                pool.tensor_tensor(xs[:, p % XSLOTS, 1, :, 0:INPUTS], by_sample(xraw, p),
                                   xs[:, p % XSLOTS, 0, :, 0:INPUTS].bitcast(f32), ALU.subtract).then_inc(xl_done, 1)

            def w1_lo(c, m):
                pool.wait_ge(w_hi, REST + MT1 * c + m + 1)
                pool.tensor_tensor(w1l[:, m % 2, :], stage[:, m % 2, :], w1h[:, m % 2, :].bitcast(f32),
                                   ALU.subtract).then_inc(w_done, 1)

            for p in range(SLICES):
                input_lo(0, p)
            for n in range(REST):
                hi, lo, cols = w23_parts(n)
                pool.wait_ge(w_hi, n + 1)
                pool.tensor_tensor(lo, stage[:, n % 2, 0:cols], hi.bitcast(f32), ALU.subtract).then_inc(w_done, 1)

            def body(c, more):
                if more:
                    for p in range(XSLOTS - 1):
                        input_lo(c + 1, p)
                w1_lo(c, 0)
                w1_lo(c, 1)
                if more:
                    input_lo(c + 1, XSLOTS - 1)
                    input_lo(c + 1, XSLOTS)
                for m in range(MT1):
                    for p in ahead(m) if more else []:
                        input_lo(c + 1, p)
                    if m + 2 < MT1:
                        w1_lo(c, m + 2)

            with pool.Fori(0, CHUNKS - 1) as c:
                body(c, True)
            body(CHUNKS - 1, False)

        @block.scalar
        def _(act):
            def grams_from_psum(g, h, first=False):
                n = HALVES * g + h
                act.wait_ge(gram_done, n + 1)
                if h % 2 == 0:
                    ge(act, half_sums, SLICES * g + h // 2 - 1)
                at = h % 2 * HALF_GROUPS
                for q in range(GROUP):
                    rows = slice(q * QUAD, (q + 1) * QUAD)
                    src = gram_banks(first, h)[rows].rearrange("p b (g t c) -> p (b g) t c", t=2, c=P)
                    last = act.activation(grams2[rows, h // 2 % 2, at:at + HALF_GROUPS, :, :],
                                          src[:, :, :, q * QUAD:q * QUAD + INPUTS], ACT.Copy)
                last.then_inc(grams_out, 1)

            def pairs_hi_part(g, s, first=False):
                act.wait_ge(pairs_t, SUBS * g + s + 1)
                dst = featH[0:PAIRS_TILE, 1:KT0, s * SUB:(s + 1) * SUB]
                src = pair_bank(first)[0:PAIRS_TILE, 0:PAIR_TILES * SUB].rearrange("p (t b) -> p t b", b=SUB)
                act.activation(dst, src, ACT.Copy).then_inc(pairs_hi, 1)

            def relu(c, layer, m, bank, more=True):
                n, row = nth(c, layer, m, more), [0, MT0, MT0 + MT1, MT0 + MT1 + MT2][layer] + m
                act.wait_ge(tile_done, n + 1)
                ge(act, split_done, n - 1)
                act.activation(act_out[:, slot(layer, m, more), :], bank, ACT.Relu, bias=bias[:, row:row + 1])\
                   .then_inc(relu_done, 1)

            def w1_hi(c, m):
                act.wait_ge(w_in[m % 2], staged(c, m))
                act.wait_ge(tile_done, nth(c, 1, m - 2) + 1 if m >= 2 else nth(c, 0, EARLY) + 1)
                act.activation(w1h[:, m % 2, :], stage[:, m % 2, :], ACT.Copy).then_inc(w_hi, 1)

            act.wait_ge(zero_done, 2)
            for h in range(HALVES):
                grams_from_psum(0, h, True)
                if h % (2 * SLICES_SUB) == 3 and h > 3:
                    pairs_hi_part(0, h // (2 * SLICES_SUB) - 1, True)
            pairs_hi_part(0, SUBS - 1, True)
            act.wait_ge(small_in, 48)
            for n in range(REST):
                hi, _, cols = w23_parts(n)
                act.wait_ge(w_in[n % 2], 16 * ((W0_LOADS + n) // 2 + 1))
                act.activation(hi, stage[:, n % 2, 0:cols], ACT.Copy).then_inc(w_hi, 1)

            def body(c, more):
                def on_half(h):
                    if more:
                        grams_from_psum(c + 1, h)
                    if h >= MT0 - FIRST_HALF + 3 and (h - MT0 + FIRST_HALF) % 4 == 3:
                        m = (h - MT0 + FIRST_HALF) // 4
                        if m + 2 < MT1:
                            w1_hi(c, m + 2)

                def on_turn(s):
                    if more:
                        pairs_hi_part(c + 1, s)

                def on_tile(layer, m):
                    relu(c, layer, m, work[:, m % 2, :])
                    if layer == 0 and m < EARLY + 2:
                        w1_hi(c, m - EARLY)

                interleave(on_half, on_turn, on_tile)
                for m in range(MT2):
                    relu(c, 2, m, acc[:, m, :])
                if more:
                    relu(c + 1, 0, 0, work[:, 0, :])
                for m in range(MT3):
                    relu(c, 3, m, acc[:, m, :], more)
                if more:
                    relu(c + 1, 0, 1, work[:, 1, :])

            for m in range(EARLY):
                relu(0, 0, m, work[:, m, :])
            with act.Fori(0, CHUNKS - 1) as c:
                body(c, True)
            body(CHUNKS - 1, False)

        @block.vector
        def _(dve):
            for i in range(XSLOTS):
                dve.memset(xs[:, i, :, :, INPUTS:].bitcast(f32), 0.0).then_inc(pads_done, 1)

            def input_hi(g, p):
                n = SLICES * g + p
                dve.wait_ge(x_in[p % XSLOTS], 16 * (SLICES // XSLOTS * g + p // XSLOTS + 1))
                ge(dve, gram_done, 2 * (n - XSLOTS + 1))
                dve.tensor_copy(xs[:, p % XSLOTS, 0, :, 0:INPUTS], by_sample(xraw, p)).then_inc(xh_done, 1)

            def dense_parts(g):
                dve.wait_ge(x0_in, 16 * (g + 1))
                dve.tensor_copy(featH[:, 0, :], x0raw[:, :]).then_inc(dense_hi, 1)
                dve.wait_ge(dense_hi, g + 1)
                dve.tensor_tensor(featL[:, 0, :], x0raw[:, :], featH[:, 0, :].bitcast(f32), ALU.subtract)\
                   .then_inc(dense_done, 1)

            def half_sum(g, p):
                n = SLICES * g + p
                dve.wait_ge(grams_out, 2 * (n + 1))
                ge(dve, turned_done, SUBS * g + p // SLICES_SUB)
                at = p % SLICES_SUB * SLICE_GROUPS
                dve.scalar_tensor_tensor(out=grams[:, at:at + SLICE_GROUPS, :], in0=grams2[:, p % 2, :, 0, :],
                                         scalar=0.5, in1=grams2[:, p % 2, :, 1, :], op0=ALU.mult, op1=ALU.add)\
                   .then_inc(half_sums, 1)

            def pair_products(g, s):
                n = SUBS * g + s
                dve.wait_ge(half_sums, SLICES_SUB * (n + 1))
                ge(dve, sums_done, 2 * n)
                dve.transpose(turned[:, :, :], grams[:, :, :].rearrange("p g m -> p m g")).then_inc(turned_done, 1)
                dve.wait_ge(turned_done, n + 1)
                ge(dve, pairs_done, n)
                full = turned[:, :, 0:INPUTS]
                dve.tensor_tensor(sums[:, 0:INPUTS * INPUTS].rearrange("p (i j) -> p i j", j=INPUTS),
                                  full, full.rearrange("p i j -> p j i"), ALU.add).then_inc(sums_done, 1)
                v = turned[:, 0, 0:APART]
                above = bass.AP(v.tensor, v.offset + APART + 1, [v.ap[0], (QUAD + 1, APART)])
                below = bass.AP(v.tensor, v.offset + QUAD * (APART + 1), [v.ap[0], (QUAD + 1, APART)])
                dve.tensor_tensor(sums[:, INPUTS * INPUTS:], above, below, ALU.add).then_inc(sums_done, 1)
                dve.wait_ge(sums_done, 2 * (n + 1))
                ge(dve, pairs_t, n)
                v = sums[:, 1:1 + APART]
                once = bass.AP(v.tensor, v.offset, [v.ap[0], (INPUTS + 1, INPUTS), (1, APART)])
                dve.tensor_copy(pairs[:, :].rearrange("p (m k) -> p m k", k=APART), once).then_inc(pairs_done, 1)

            def half_point(g, h):
                p = h // 2
                if h % 2 == 0:
                    if p + XSLOTS - 1 < SLICES:
                        input_hi(g, p + XSLOTS - 1)
                else:
                    half_sum(g, p)
                    if p % SLICES_SUB == SLICES_SUB - 1:
                        pair_products(g, p // SLICES_SUB)

            def pairs_lo_part(g, s, first=False):
                dve.wait_ge(pairs_hi, SUBS * g + s + 1)
                at = slice(s * SUB, (s + 1) * SUB)
                src = pair_bank(first)[0:PAIRS_TILE, 0:PAIR_TILES * SUB].rearrange("p (t b) -> p t b", b=SUB)
                dve.tensor_tensor(featL[0:PAIRS_TILE, 1:KT0, at], src, featH[0:PAIRS_TILE, 1:KT0, at].bitcast(f32),
                                  ALU.subtract).then_inc(pairs_lo, 1)

            def split(c, layer, m, hi, lo, more=True):
                n, full = nth(c, layer, m, more), act_out[:, slot(layer, m, more), :]
                dve.wait_ge(relu_done, n + 1)
                dve.tensor_copy(hi, full).then_inc(hi_done, 1)
                dve.wait_ge(hi_done, n + 1)
                dve.tensor_tensor(lo, full, hi.bitcast(f32), ALU.subtract).then_inc(split_done, 1)

            def w0_parts(n):
                dve.wait_ge(w_in[n % 2], 16 * (n // 2 + 1))
                dve.tensor_copy(w0h[:, n, :], stage[:, n % 2, :]).then_inc(w0_hi, 1)
                dve.wait_ge(w0_hi, n + 1)
                dve.tensor_tensor(w0l[:, n, :], stage[:, n % 2, :], w0h[:, n, :].bitcast(f32), ALU.subtract)\
                   .then_inc(w0_done, 1)

            dve.wait_ge(pads_done, XSLOTS)
            for p in range(XSLOTS - 1):
                input_hi(0, p)
            dve.memset(featH[:, KT0 - 1, :].bitcast(f32), 0.0).then_inc(zero_done, 1)
            dve.memset(featL[:, KT0 - 1, :].bitcast(f32), 0.0).then_inc(zero_done, 1)
            for h in range(HALVES):
                half_point(0, h)
                if h % (2 * SLICES_SUB) == 3 and h > 3:
                    pairs_lo_part(0, h // (2 * SLICES_SUB) - 1, True)
                if h % 8 == 6:
                    w0_parts(h // 8)
            dense_parts(0)
            dve.wait_ge(small_in, 48)
            dve.tensor_copy(w4s[:, :, 0:1], w4raw[:, :, :]).then_inc(w4_hi, 1)
            dve.wait_ge(w4_hi, 1)
            dve.tensor_tensor(w4s[:, :, 1:2], w4raw[:, :, :], w4s[:, :, 0:1].bitcast(f32), ALU.subtract)\
               .then_inc(w4_done, 1)
            pairs_lo_part(0, SUBS - 1, True)

            def body(c, more):
                def on_half(h):
                    if more:
                        half_point(c + 1, h)

                def on_turn(s):
                    if more:
                        pairs_lo_part(c + 1, s)

                def on_tile(layer, m):
                    if layer == 0:
                        split(c, 0, m, h1h[:, m, :], h1l[:, m, :])
                        if more and m < EARLY + XSLOTS - 1:
                            input_hi(c + 1, m - EARLY)
                    else:
                        split(c, 1, m, h2h[:, m % 2, :], h2l[:, m % 2, :])
                        if more and m == 0:
                            dense_parts(c + 1)

                interleave(on_half, on_turn, on_tile)
                for m in range(MT2):
                    split(c, 2, m, h1h[:, H3 + m, :], h1l[:, H3 + m, :])
                if more:
                    split(c + 1, 0, 0, h1h[:, 0, :], h1l[:, 0, :])
                for m in range(MT3):
                    split(c, 3, m, h2h[:, m, :], h2l[:, m, :], more)
                if more:
                    split(c + 1, 0, 1, h1h[:, 1, :], h1l[:, 1, :])
                dve.wait_ge(logits_done, c + 1)
                dve.tensor_reduce(ysum[:, :], acc[:, 3, 0:2 * SUBS].rearrange("p (s t) -> p s t", t=2),
                                  mybir.AxisListType.X, ALU.add).then_inc(ysum_done, 1)
                dve.wait_ge(ysum_done, c + 1)
                at = slice(c * SUBS, (c + 1) * SUBS) if isinstance(c, int) else bass.ts(c, SUBS)
                dve.tensor_scalar(y[:, at], ysum[:, :], bias4[:, 0:1], None, ALU.add).then_inc(y_done, 1)

            for m in range(EARLY):
                split(0, 0, m, h1h[:, m, :], h1l[:, m, :])
            with dve.Fori(0, CHUNKS - 1) as c:
                body(c, True)
            body(CHUNKS - 1, False)

        @block.tensor
        def _(pe):
            def product(dst, wh, wl, ah, al, start, stop):
                pe.matmul(dst, wl, ah, start=start, stop=False)
                pe.matmul(dst, wh, ah, start=False, stop=False)
                return pe.matmul(dst, wh, al, start=False, stop=stop)

            def gram_half(g, h, turned_before, first=False):
                n, p = HALVES * g + h, h // 2
                pe.wait_ge(xh_done, SLICES * g + p + 1)
                pe.wait_ge(xl_done, SLICES * g + p + 1)
                ge(pe, grams_out, n - 1 if first else n)
                if not first:
                    pe.wait_ge(pairs_lo, SUBS * g + turned_before)
                banks = gram_banks(first, h)
                for j in range(HALF_GROUPS):
                    k = h % 2 * HALF_GROUPS + j
                    four = slice(k * GROUP, (k + 1) * GROUP)
                    last = pe.matmul(banks[:, j // 2, j % 2 * 2 * P:(j % 2 + 1) * 2 * P],
                                     xs[:, p % XSLOTS, 0, four, :].rearrange("p b n -> p (b n)"),
                                     xs[:, p % XSLOTS, :, four, :].rearrange("p t b n -> p t (b n)"),
                                     start=True, stop=True)
                last.then_inc(gram_done, 1)

            def transpose_pairs(g, s, halves_before, first=False):
                pe.wait_ge(pairs_done, SUBS * g + s + 1)
                if first:
                    ge(pe, pairs_lo, s)
                else:
                    pe.wait_ge(grams_out, HALVES * g + halves_before)
                for t in range(PAIR_TILES):
                    last = pe.transpose(pair_bank(first)[0:PAIRS_TILE, t * SUB:(t + 1) * SUB],
                                        pairs[:, t * PAIRS_TILE:(t + 1) * PAIRS_TILE], ident[:, :])
                last.then_inc(pairs_t, 1)

            def layer0(c, m):
                if m == 0:
                    pe.wait_ge(dense_done, c + 1)
                    pe.wait_ge(pairs_lo, SUBS * (c + 1))
                if m >= EARLY:
                    pe.wait_ge(relu_done, nth(c, 0, m) - 1)
                cols = slice(m * P, (m + 1) * P)
                for k in range(KT0):
                    rows = slice(0, P if k == 0 else PAIRS_TILE if k < KT0 - 1 else ZERO_ROW + 1)
                    last = product(work[:, m % 2, :], w0h[rows, k, cols], w0l[rows, k, cols],
                                   featH[rows, k, :], featL[rows, k, :], k == 0, k == KT0 - 1)
                last.then_inc(tile_done, 1)

            def layer1(c, m, k):
                if k == 0:
                    pe.wait_ge(w_done, REST + MT1 * c + m + 1)
                    pe.wait_ge(relu_done, nth(c, 1, m) - 1)
                if m == 0:
                    pe.wait_ge(split_done, nth(c, 0, max(k, EARLY)) + (k >= EARLY))
                cols = slice(k * P, (k + 1) * P)
                last = product(work[:, m % 2, :], w1h[:, m % 2, cols], w1l[:, m % 2, cols],
                               h1h[:, k, :], h1l[:, k, :], k == 0, k == KT1 - 1)
                if k == KT1 - 1:
                    last.then_inc(tile_done, 1)

            def layer2(c, k, ms):
                pe.wait_ge(split_done, nth(c, 1, k) + 1)
                for m in ms:
                    cols = slice(k * SIZES[2] + m * P, k * SIZES[2] + (m + 1) * P)
                    last = product(acc[:, m, :], w2h[:, cols], w2l[:, cols], h2h[:, k % 2, :], h2l[:, k % 2, :],
                                   k == 0, k == KT2 - 1)
                    if k == KT2 - 1:
                        last.then_inc(tile_done, 1)

            def layer3(c, m, more):
                for k in range(KT3):
                    if m == 0:
                        pe.wait_ge(split_done, nth(c, 2, k) + 1)
                    cols = slice(k * SIZES[3] + m * P, k * SIZES[3] + (m + 1) * P)
                    last = product(acc[:, m, :], w3h[:, cols], w3l[:, cols], h1h[:, H3 + k, :], h1l[:, H3 + k, :],
                                   k == 0, k == KT3 - 1)
                last.then_inc(tile_done, 1)

            def layer4(c, more):
                for k in range(MT3):
                    pe.wait_ge(split_done, nth(c, 3, k, more) + 1)
                for s in range(SUBS):
                    for k in range(MT3):
                        at = slice(s * SUB, (s + 1) * SUB)
                        dst = acc[:, 3, 2 * s:2 * s + 2]
                        pe.matmul(dst, h2h[:, k, at], w4s[:, k, :], start=k == 0, stop=False)
                        last = pe.matmul(dst, h2l[:, k, at], w4s[:, k, :], start=False, stop=k == MT3 - 1)
                last.then_inc(logits_done, 1)

            pe.wait_ge(pads_done, XSLOTS)
            pe.wait_ge(ident_done, 1)
            for h in range(HALVES):
                gram_half(0, h, 0, True)
                if h % (2 * SLICES_SUB) == 3 and h > 3:
                    transpose_pairs(0, h // (2 * SLICES_SUB) - 1, 0, True)
            transpose_pairs(0, SUBS - 1, 0, True)
            pe.wait_ge(w0_done, W0_LOADS)
            pe.wait_ge(w4_done, 1)

            for m in range(EARLY):
                layer0(0, m)

            def body(c, more):
                for m in range(EARLY, MT0):
                    layer0(c, m)
                    if more and m >= FIRST_HALF:
                        gram_half(c + 1, m - FIRST_HALF, 0)
                for m in range(MT1):
                    for k in range(KT1):
                        layer1(c, m, k)
                        if more and (m, k) in IN_L1:
                            gram_half(c + 1, IN_L1[m, k], m // 2 + (m % 2 and k > TURN_AT_K))
                        if more and m % 2 and k == TURN_AT_K:
                            transpose_pairs(c + 1, m // 2, IN_L1.get((m, 2), HALVES - 1) + 1)
                    if m:
                        if m == 1:
                            pe.wait_ge(w_done, W2_LOADS)
                        layer2(c, m - 1, range(MT2 // 2))
                        if more and (m, KT1) in IN_L1:
                            gram_half(c + 1, IN_L1[m, KT1], (m + 1) // 2)
                        layer2(c, m - 1, range(MT2 // 2, MT2))
                layer2(c, KT2 - 1, range(MT2))
                if more:
                    layer0(c + 1, 0)
                pe.wait_ge(w_done, REST)
                for m in range(MT3):
                    layer3(c, m, more)
                if more:
                    layer0(c + 1, 1)
                layer4(c, more)

            with pe.Fori(0, CHUNKS - 1) as c:
                body(c, True)
            body(CHUNKS - 1, False)


def kernel(**inputs):
    import concourse.bacc as _bacc
    from concourse.bass_utils import run_bass_kernel_spmd as _run

    x = np.ascontiguousarray(inputs["r_bottom_output"])
    W = [np.ascontiguousarray(inputs[f"L0_rec_W{i}"]) for i in range(5)]
    b = [np.ascontiguousarray(inputs[f"L0_rec_b{i}"]) for i in range(5)]

    xs = x.reshape(GROUP, QUAD, CHUNKS * SUBS, INPUTS, EMB)
    x_t = xs.transpose(2, 1, 0, 3, 4).reshape(CHUNKS * SLICES, SLICE_GROUPS * GROUP * INPUTS, EMB).transpose(0, 2, 1)
    x0_t = x[:, 0, :].reshape(P, CHUNKS, SUBS, EMB).transpose(1, 3, 2, 0).reshape(CHUNKS, EMB, CHUNK)

    rows = pair_features()
    w0 = np.zeros((KT0, P, SIZES[0]), W[0].dtype)
    w0[rows >= 0] = W[0].T[rows[rows >= 0]]
    w1 = W[1].reshape(MT1, P, KT1, P).transpose(0, 3, 2, 1).reshape(MT1, P, KT1 * P)
    w2 = W[2].T.reshape(KT2, P, SIZES[2]).transpose(1, 0, 2).reshape(P, W2_LOADS, STAGE).transpose(1, 0, 2)
    w3 = W[3].T.reshape(KT3, P, SIZES[3]).transpose(1, 0, 2).reshape(P, W3_LOADS, KT3 * SIZES[3] // W3_LOADS).transpose(1, 0, 2)
    w4 = W[4].reshape(MT3, P, 1).transpose(1, 0, 2)
    biases = np.concatenate([v.reshape(-1, P) for v in b[:4]]).T

    nc = _bacc.Bacc("TRN2", target_bir_lowering=False, num_devices=1, dynamic_dma_scratch_size=1024)
    arrays = {}

    def given(name, a):
        arrays[name] = np.ascontiguousarray(a)
        return nc.dram_tensor(name, arrays[name].shape, mybir.dt.from_np(a.dtype), kind="ExternalInput").ap()

    args = [given("x_t", x_t), given("x0_t", x0_t), given("w0_t", w0), given("w1_t", w1), given("w2_t", w2),
            given("w3_t", w3), given("w4_t", w4), given("biases", biases), given("b4", b[4].reshape(1, 1))]
    out = nc.dram_tensor("out_0", (BATCH, 1), mybir.dt.float32, kind="ExternalOutput").ap()
    rec_program(nc, *args, out.rearrange("(p t) a -> p (t a)", p=P))
    r = _run(nc, [arrays], core_ids=[0])
    return r.results[0]["out_0"]
```

```python
import numpy as np
import concourse.bass as bass
from concourse import mybir
from contextlib import ExitStack

BATCH, INPUTS, EMB = 2048, 27, 128
SIZES = [1024, 1024, 512, 256]
P = 128
CHUNK = 512
CHUNKS = BATCH // CHUNK
SUB = 128
SUBS = CHUNK // SUB
GROUP = 4
QUAD = P // GROUP
SLICE_GROUPS = 8
HALF_GROUPS = SLICE_GROUPS // 2
SCOLS = SLICE_GROUPS * GROUP * INPUTS
BANK = 512
SLICES_SUB = SUB // (GROUP * SLICE_GROUPS)
SLICES = SUBS * SLICES_SUB
HALVES = 2 * SLICES
APART = (INPUTS - 1) // 2
PAIR_TILES = 3
M_TILE = INPUTS // PAIR_TILES
PAIRS_TILE = M_TILE * APART
KT0 = 1 + PAIR_TILES
ZERO_ROW = PAIRS_TILE
XSLOTS = 4
KT1, KT2, KT3 = SIZES[0] // P, SIZES[1] // P, SIZES[2] // P
MT0, MT1, MT2, MT3 = (s // P for s in SIZES)
TILES = MT0 + MT1 + MT2 + MT3
LOAD = 1024
W0_LOADS = KT0
W2_LOADS = KT2 * SIZES[2] // LOAD
REST = W2_LOADS + 1
assert SIZES[0] == KT1 * P == KT3 * SIZES[3] == LOAD and MT1 % 2 == 0 and SLICES % XSLOTS == 0


def pair_features():
    rows = np.full((KT0, P), -1)
    rows[0] = np.arange(EMB)
    for t in range(PAIR_TILES):
        for i in range(PAIRS_TILE):
            m, k = M_TILE * t + i // APART, 1 + i % APART
            flat = (INPUTS + 1) * m + k
            if m == INPUTS - 1:
                r, c = k - 1, k + APART
            else:
                r, c = flat // INPUTS, flat % INPUTS
            hi, lo = max(r, c), min(r, c)
            rows[1 + t, i] = EMB + hi * (hi - 1) // 2 + lo
    rows[KT0 - 1, ZERO_ROW] = EMB + INPUTS * (INPUTS - 1) // 2
    return rows


def rec_program(nc, x_t, x0_t, w0, w1, w2, w3, w4, biases, b4, out):
    f32, f32r = mybir.dt.float32, mybir.dt.float32r
    ALU = mybir.AluOpType
    ACT = mybir.ActivationFunctionType

    ctx = ExitStack()
    with ctx:
        def sb(name, shape, dt=f32):
            return ctx.enter_context(nc.sbuf_tensor(name, shape, dt))

        def sem(name):
            return ctx.enter_context(nc.semaphore(name))

        with nc.sbuf_tensor("w0raw", [P, KT0, SIZES[0]], f32) as w0raw, \
                nc.sbuf_tensor("w2raw", [P, KT2 * SIZES[2]], f32) as w2raw, \
                nc.sbuf_tensor("w3raw", [P, KT3 * SIZES[3]], f32) as w3raw:
            pass
        w0l, w2l = sb("w0l", [P, KT0, SIZES[0]], f32r), sb("w2l", [P, KT2 * SIZES[2]], f32r)
        w3l = sb("w3l", [P, KT3 * SIZES[3]], f32r)
        w0h, w2h = sb("w0h", [P, KT0, SIZES[0]], f32r), sb("w2h", [P, KT2 * SIZES[2]], f32r)
        w3h = sb("w3h", [P, KT3 * SIZES[3]], f32r)
        w1h, w1l = sb("w1h", [P, 2, KT1 * P], f32r), sb("w1l", [P, 2, KT1 * P], f32r)
        w4raw = sb("w4raw", [P, MT3, 1])
        w4s = sb("w4s", [P, MT3, 2], f32r)
        stage = sb("stage", [P, 2, LOAD])
        bias = sb("bias", [P, MT0 + MT1 + MT2 + MT3])
        bias4 = sb("bias4", [P, 1])
        ident = sb("ident", [P, P])

        xraw = sb("xraw", [P, XSLOTS, SCOLS])
        with nc.sbuf_tensor("xpad", [P, 2 * XSLOTS, SLICE_GROUPS * GROUP, QUAD], f32) as xpad:
            pass
        xs = sb("xs", [P, XSLOTS, 2, SLICE_GROUPS * GROUP, QUAD], f32r)
        x0raw = sb("x0raw", [P, CHUNK])
        grams2 = sb("grams2", [P, 2, SLICE_GROUPS, 2, INPUTS])
        grams = sb("grams", [P, SUB // GROUP, INPUTS])
        turned = sb("turned", [P, INPUTS, QUAD])
        sums = sb("sums", [P, INPUTS * INPUTS + APART])
        pairs = sb("pairs", [P, PAIR_TILES * PAIRS_TILE])
        featH, featL = sb("featH", [P, KT0, CHUNK], f32r), sb("featL", [P, KT0, CHUNK], f32r)
        h1h, h1l = sb("h1h", [P, MT0, CHUNK], f32r), sb("h1l", [P, MT0, CHUNK], f32r)
        h2h, h2l = sb("h2h", [P, 2, CHUNK], f32r), sb("h2l", [P, 2, CHUNK], f32r)
        act_out = sb("act_out", [P, 2, CHUNK])
        ysum = sb("ysum", [P, SUBS])
        y = sb("y", [P, CHUNKS * SUBS])
        H3 = MT0 - MT2

        work = ctx.enter_context(nc.psum_tensor("work", [P, 2, BANK], f32))
        acc = ctx.enter_context(nc.psum_tensor("acc", [P, 4, BANK], f32))
        gps = ctx.enter_context(nc.psum_tensor("gps", [P, 2, BANK], f32))

        small_in = sem("small_in")
        w0_in, w23_in = [sem(f"w0_in{n}") for n in range(W0_LOADS)], [sem(f"w23_in{n}") for n in range(REST)]
        w_in = [sem(f"w_in{i}") for i in range(2)]
        x_in = [sem(f"x_in{i}") for i in range(XSLOTS)]
        x0_in = sem("x0_in")
        ident_zero, ident_done, zero_done = sem("ident_zero"), sem("ident_done"), sem("zero_done")
        xpads_zero, pads_done = sem("xpads_zero"), sem("pads_done")
        w0_hi, w0_done = sem("w0_hi"), sem("w0_done")
        w_hi, w_done = sem("w_hi"), sem("w_done")
        w4_hi, w4_done = sem("w4_hi"), sem("w4_done")
        xpad_done = sem("xpad_done")
        xh_done, xl_done = sem("xh_done"), sem("xl_done")
        gram_done, grams_out, half_sums = sem("gram_done"), sem("grams_out"), sem("half_sums")
        turned_done, sums_done, pairs_done = sem("turned_done"), sem("sums_done"), sem("pairs_done")
        pairs_t, pairs_hi, pairs_lo = sem("pairs_t"), sem("pairs_hi"), sem("pairs_lo")
        dense_hi, dense_done = sem("dense_hi"), sem("dense_done")
        left_done, left_relu = sem("left_done"), sem("left_relu")
        left_hi, left_split = sem("left_hi"), sem("left_split")
        tile_done, relu_done = sem("tile_done"), sem("relu_done")
        hi_done, split_done = sem("hi_done"), sem("split_done")
        logits_done, ysum_done, y_done, out_done = sem("logits_done"), sem("ysum_done"), sem("y_done"), sem("out_done")

        def ge(eng, s, value):
            if not (isinstance(value, int) and value <= 0):
                eng.wait_ge(s, value)

        def at_first(c):
            return isinstance(c, int) and c == 0

        def by_sample(buf, p):
            return buf[:, p % XSLOTS, :].rearrange("p (b n) -> p b n", n=INPUTS)

        def w23(n):
            if n == W2_LOADS:
                return w3raw[:, :], w3h[:, :], w3l[:, :]
            cols = slice(n * LOAD, (n + 1) * LOAD)
            return w2raw[:, cols], w2h[:, cols], w2l[:, cols]

        def parts(g, p):
            return SLICES * (g - 1) + p + 1

        def staged(c, m):
            return 16 * (MT1 // 2 * c + m // 2 + 1)

        EARLY = 2

        def nth(c, layer, m, more=True):
            if layer == 0 and m < EARLY:
                return m if at_first(c) else TILES * c + (m - EARLY if m == 0 else m)
            first = {0: 0, 1: MT0, 2: MT0 + MT1, 3: MT0 + MT1 + MT2 + (1 if more else 0)}
            return TILES * c + first[layer] + m

        def slot(layer, m, more=True):
            return nth(0, layer, m, more) % 2 if (layer, m) != (0, 1) else 1

        FIRST_HALF = MT0 // 2
        places = [(0, 2), (0, 5)]
        for m in range(1, MT1 - 1):
            places += [(m, k) for k in ([0, 2, 6, KT1] if m % 2 == 0 else [0, 3, 6, KT1])]
        places += [(MT1 - 1, 0), (MT1 - 1, 3)]
        IN_L1 = {place: MT0 - FIRST_HALF + h for h, place in enumerate(places)}
        TURNS = {(2, 4): 0, (4, 4): 1, (6, 4): 2, (MT1 - 1, KT1): 3}
        assert MT0 - FIRST_HALF + len(places) == HALVES and len(TURNS) == SUBS

        def before(place):
            return (MT0 - FIRST_HALF + sum(p < place for p in IN_L1), sum(p < place for p in TURNS))

        LEFT, RIGHT = slice(0, CHUNK // 2), slice(CHUNK // 2, CHUNK)
        W0_AFTER = [1, 3, 5, 7]
        W23_AFTER = [11, 12, 13, 14, 15]
        HI_BEHIND = 2
        PAD_AHEAD = 2
        TRANSPOSE_AT = SLICES_SUB + 2
        LEFT_AT = 2 * SLICES_SUB + 4
        LEFT_AFTER = SLICES - LEFT_AT

        def columns(c):
            return RIGHT if at_first(c) else slice(0, CHUNK)

        def ahead(m):
            return range(2 * m + XSLOTS + 1, min(2 * m + XSLOTS + 3, SLICES))

        def pair_bank(first):
            return acc[:, 2, :] if first else gps[:, 0, :]

        def first_banks(p):
            return acc[:, 0:2, :] if p % 2 else gps[:, :, :]

        def first_grams(s):
            return grams2[:, :, :, :, :].rearrange("p a g t n -> p (a g t) n") if s % 2 else grams[:, :, :]

        block = ctx.enter_context(nc.Block())

        def interleave(on_half, on_turn, on_tile, after_tile):
            for m in range(EARLY, MT0):
                on_tile(0, m)
                if m >= FIRST_HALF:
                    on_half(m - FIRST_HALF)
            for m in range(MT1):
                for k in range(KT1 + 1):
                    if (m, k) in IN_L1:
                        on_half(IN_L1[m, k])
                    if (m, k) in TURNS:
                        on_turn(TURNS[m, k])
                    if k == KT1 - 1:
                        on_tile(1, m)
                after_tile(m)

        @block.sync
        def _(sp):
            def load_x(g, p):
                n = SLICES * g + p
                if isinstance(g, int) and n < SLICES + XSLOTS:
                    ge(sp, xpad_done, n - XSLOTS + 1)
                elif p < XSLOTS:
                    sp.wait_ge(gram_done, 2 * (n - XSLOTS + 1))
                else:
                    sp.wait_ge(xl_done, parts(g, p - XSLOTS))
                sp.dma_start(xraw[:, p % XSLOTS, :], x_t[n, :, :]).then_inc(x_in[p % XSLOTS], 16)

            def load_x0(g):
                ge(sp, dense_done, g)
                sp.dma_start(x0raw[:, :], x0_t[g, :, :]).then_inc(x0_in, 16)

            def load_w1(c, m):
                if not (at_first(c) and m < 2):
                    sp.wait_ge(w_done, REST + MT1 * c + m - 1)
                sp.dma_start(stage[:, m % 2, :], w1[m, :, :]).then_inc(w_in[m % 2], 16)

            load_x(0, 0)
            sp.dma_start(w4raw[:, :, :], w4).then_inc(small_in, 16)
            sp.dma_start(bias[:, :], biases).then_inc(small_in, 16)
            sp.dma_start(bias4[:, :], b4.to_broadcast([P, 1])).then_inc(small_in, 16)
            for p in range(1, SLICES):
                load_x(0, p)
                if p in W0_AFTER:
                    n = W0_AFTER.index(p)
                    sp.dma_start(w0raw[:, n, :], w0[n, :, :]).then_inc(w0_in[n], 16)
                if p == W0_AFTER[-1] + 1:
                    load_x0(0)
                if p in W23_AFTER:
                    n = W23_AFTER.index(p)
                    sp.dma_start(w23(n)[0], w2[n, :, :] if n < W2_LOADS else w3).then_inc(w23_in[n], 16)

            def body(c, more):
                if more:
                    load_x0(c + 1)
                    for p in range(XSLOTS):
                        load_x(c + 1, p)
                load_w1(c, 0)
                load_w1(c, 1)
                if more:
                    load_x(c + 1, XSLOTS)
                for m in range(MT1):
                    for p in ahead(m) if more else []:
                        load_x(c + 1, p)
                    if m + 2 < MT1:
                        load_w1(c, m + 2)

            body(0, True)
            with sp.Fori(1, CHUNKS - 1) as c:
                body(c, True)
            body(CHUNKS - 1, False)
            sp.wait_ge(y_done, CHUNKS)
            sp.dma_start(out, y[:, :]).then_inc(out_done, 16)
            sp.wait_ge(out_done, 16)

        @block.gpsimd
        def _(pool):
            pool.memset(ident[:, :], 0.0).then_inc(ident_zero, 1)
            pool.wait_ge(ident_zero, 1)
            pool.affine_select(out=ident[:, :], in_=ident[:, :], compare_op=ALU.not_equal, fill=1.0, base=0,
                               pattern=[[-1, P]], channel_multiplier=1).then_inc(ident_done, 1)

            def input_lo(g, p):
                n = SLICES * g + p
                pool.wait_ge(xh_done, parts(g, p))
                ge(pool, gram_done, 2 * (n - XSLOTS + 1))
                pool.tensor_tensor(xs[:, p % XSLOTS, 1, :, 0:INPUTS], by_sample(xraw, p),
                                   xs[:, p % XSLOTS, 0, :, 0:INPUTS].bitcast(f32), ALU.subtract).then_inc(xl_done, 1)

            def w1_lo(c, m):
                pool.wait_ge(w_hi, REST + MT1 * c + m + 1)
                pool.tensor_tensor(w1l[:, m % 2, :], stage[:, m % 2, :], w1h[:, m % 2, :].bitcast(f32),
                                   ALU.subtract).then_inc(w_done, 1)

            for n in range(W0_LOADS):
                pool.wait_ge(w0_hi, n + 1)
                pool.tensor_tensor(w0l[:, n, :], w0raw[:, n, :], w0h[:, n, :].bitcast(f32), ALU.subtract)\
                    .then_inc(w0_done, 1)

            def w23_lo(n):
                raw, hi, lo = w23(n)
                pool.wait_ge(w_hi, n + 1)
                pool.tensor_tensor(lo, raw, hi.bitcast(f32), ALU.subtract).then_inc(w_done, 1)

            for n in range(REST - 1):
                w23_lo(n)
            pool.wait_ge(gram_done, 2 * SLICES)
            for i in range(XSLOTS):
                pool.memset(xs[:, i, :, :, INPUTS:].bitcast(f32), 0.0).then_inc(pads_done, 1)
            input_lo(1, 0)
            input_lo(1, 1)
            w23_lo(REST - 1)
            input_lo(1, 2)

            def body(c, more):
                if more and not at_first(c):
                    for p in range(XSLOTS - 1):
                        input_lo(c + 1, p)
                w1_lo(c, 0)
                w1_lo(c, 1)
                if more:
                    input_lo(c + 1, XSLOTS - 1)
                    input_lo(c + 1, XSLOTS)
                for m in range(MT1):
                    for p in ahead(m) if more else []:
                        input_lo(c + 1, p)
                    if m + 2 < MT1:
                        w1_lo(c, m + 2)

            body(0, True)
            with pool.Fori(1, CHUNKS - 1) as c:
                body(c, True)
            body(CHUNKS - 1, False)

        @block.scalar
        def _(act):
            def grams_from_psum(g, h):
                n = HALVES * g + h
                act.wait_ge(gram_done, n + 1)
                if h % 2 == 0 and h >= 4:
                    act.wait_ge(half_sums, SLICES * (g - 1) + h // 2 - 1)
                at = h % 2 * HALF_GROUPS
                for q in range(GROUP):
                    rows = slice(q * QUAD, (q + 1) * QUAD)
                    src = gps[rows].rearrange("p b (g t c) -> p (b g) t c", t=2, c=P)
                    last = act.activation(grams2[rows, h // 2 % 2, at:at + HALF_GROUPS, :, :],
                                          src[:, :, :, q * QUAD:q * QUAD + INPUTS], ACT.Copy)
                last.then_inc(grams_out, 1)

            def first_from_psum(p):
                act.wait_ge(gram_done, 2 * (p + 1))
                s = p // SLICES_SUB
                if p % SLICES_SUB == 0:
                    ge(act, turned_done, s - 1)
                at = p % SLICES_SUB * SLICE_GROUPS
                for q in range(GROUP):
                    rows = slice(q * QUAD, (q + 1) * QUAD)
                    src = first_banks(p)[rows, :, 0:HALF_GROUPS * GROUP * INPUTS]
                    src = src.rearrange("p b (g c) -> p b g c", c=GROUP * INPUTS)
                    dst = first_grams(s)[rows, at:at + SLICE_GROUPS, :].rearrange("p (b g) n -> p b g n", b=2)
                    last = act.activation(dst, src[:, :, :, q * INPUTS:(q + 1) * INPUTS], ACT.Copy)
                last.then_inc(grams_out, 2)

            def pairs_hi_part(g, s, first=False):
                act.wait_ge(pairs_t, SUBS * g + s + 1)
                dst = featH[0:PAIRS_TILE, 1:KT0, s * SUB:(s + 1) * SUB]
                src = pair_bank(first)[0:PAIRS_TILE, 0:PAIR_TILES * SUB].rearrange("p (t b) -> p t b", b=SUB)
                act.activation(dst, src, ACT.Copy).then_inc(pairs_hi, 1)

            def relu(c, layer, m, bank, more=True):
                n, row = nth(c, layer, m, more), [0, MT0, MT0 + MT1, MT0 + MT1 + MT2][layer] + m
                act.wait_ge(tile_done, n + 1)
                ge(act, split_done, n - 1)
                cols = columns(c) if layer == 0 else slice(0, CHUNK)
                act.activation(act_out[:, slot(layer, m, more), cols], bank[:, cols], ACT.Relu,
                               bias=bias[:, row:row + 1]).then_inc(relu_done, 1)

            def relu_left(m):
                act.wait_ge(left_done, m + 1)
                ge(act, left_split, m - 1)
                act.activation(act_out[:, m % 2, LEFT], work[:, m % 2, LEFT], ACT.Relu, bias=bias[:, m:m + 1])\
                   .then_inc(left_relu, 1)

            def w0_hi_part(n):
                act.wait_ge(w0_in[n], 16)
                act.activation(w0h[:, n, :], w0raw[:, n, :], ACT.Copy).then_inc(w0_hi, 1)

            def w23_hi(n):
                act.wait_ge(w23_in[n], 16)
                raw, hi, _ = w23(n)
                act.activation(hi, raw, ACT.Copy).then_inc(w_hi, 1)

            def w1_hi(c, m):
                act.wait_ge(w_in[m % 2], staged(c, m))
                act.wait_ge(tile_done, nth(c, 1, m - 2) + 1 if m >= 2 else nth(c, 0, EARLY) + 1)
                act.activation(w1h[:, m % 2, :], stage[:, m % 2, :], ACT.Copy).then_inc(w_hi, 1)

            act.wait_ge(small_in, 48)
            act.activation(w4s[:, :, 0:1], w4raw[:, :, :], ACT.Copy).then_inc(w4_hi, 1)
            act.wait_ge(zero_done, 2)
            for p in range(SLICES):
                first_from_psum(p)
                if p >= TRANSPOSE_AT and (p - TRANSPOSE_AT) % SLICES_SUB == 0:
                    pairs_hi_part(0, (p - TRANSPOSE_AT) // SLICES_SUB, True)
                if p - HI_BEHIND in W0_AFTER:
                    w0_hi_part(W0_AFTER.index(p - HI_BEHIND))
                if p >= LEFT_AT:
                    relu_left(p - LEFT_AT)
                if p - HI_BEHIND in W23_AFTER:
                    w23_hi(W23_AFTER.index(p - HI_BEHIND))
            w23_hi(REST - 2)
            for m in range(LEFT_AFTER, MT0 - 1):
                relu_left(m)
            pairs_hi_part(0, SUBS - 1, True)
            relu_left(MT0 - 1)
            w23_hi(REST - 1)

            def body(c, more):
                def on_half(h):
                    if more:
                        grams_from_psum(c + 1, h)

                def on_turn(s):
                    if more:
                        pairs_hi_part(c + 1, s)

                def on_tile(layer, m):
                    relu(c, layer, m, work[:, m % 2, :])
                    if layer == 0 and m < EARLY + 2:
                        w1_hi(c, m - EARLY)

                def after_tile(m):
                    if m + 2 < MT1:
                        w1_hi(c, m + 2)

                interleave(on_half, on_turn, on_tile, after_tile)
                for m in range(MT2):
                    relu(c, 2, m, acc[:, m, :])
                if more:
                    relu(c + 1, 0, 0, work[:, 0, :])
                for m in range(MT3):
                    relu(c, 3, m, acc[:, m, :], more)
                if more:
                    relu(c + 1, 0, 1, work[:, 1, :])

            for m in range(EARLY):
                relu(0, 0, m, work[:, m, :])
            body(0, True)
            with act.Fori(1, CHUNKS - 1) as c:
                body(c, True)
            body(CHUNKS - 1, False)

        @block.vector
        def _(dve):
            for i in range(XSLOTS):
                dve.memset(xpad[:, 2 * i:2 * i + 2, :, INPUTS:], 0.0).then_inc(xpads_zero, 1)

            def input_hi(g, p):
                n = SLICES * g + p
                dve.wait_ge(x_in[p % XSLOTS], 16 * (SLICES // XSLOTS * g + p // XSLOTS + 1))
                ge(dve, gram_done, 2 * (n - XSLOTS + 1))
                dve.tensor_copy(xs[:, p % XSLOTS, 0, :, 0:INPUTS], by_sample(xraw, p)).then_inc(xh_done, 1)

            def dense_parts(g):
                dve.wait_ge(x0_in, 16 * (g + 1))
                dve.tensor_copy(featH[:, 0, :], x0raw[:, :]).then_inc(dense_hi, 1)
                dve.wait_ge(dense_hi, g + 1)
                dve.tensor_tensor(featL[:, 0, :], x0raw[:, :], featH[:, 0, :].bitcast(f32), ALU.subtract)\
                   .then_inc(dense_done, 1)

            def half_sum(g, p):
                n = SLICES * g + p
                dve.wait_ge(grams_out, 2 * (n + 1))
                ge(dve, turned_done, SUBS * g + p // SLICES_SUB)
                at = p % SLICES_SUB * SLICE_GROUPS
                dve.scalar_tensor_tensor(out=grams[:, at:at + SLICE_GROUPS, :], in0=grams2[:, p % 2, :, 0, :],
                                         scalar=0.5, in1=grams2[:, p % 2, :, 1, :], op0=ALU.mult, op1=ALU.add)\
                   .then_inc(half_sums, 1)

            def choose_pairs(n):
                dve.wait_ge(sums_done, 2 * (n + 1))
                ge(dve, pairs_t, n)
                v = sums[:, 1:1 + APART]
                once = bass.AP(v.tensor, v.offset, [v.ap[0], (INPUTS + 1, INPUTS), (1, APART)])
                dve.tensor_copy(pairs[:, :].rearrange("p (m k) -> p m k", k=APART), once).then_inc(pairs_done, 1)

            def first_pairs(s):
                dve.wait_ge(grams_out, 2 * SLICES_SUB * (s + 1))
                ge(dve, sums_done, 2 * s)
                dve.transpose(turned[:, :, :], first_grams(s).rearrange("p g m -> p m g")).then_inc(turned_done, 1)
                dve.wait_ge(turned_done, s + 1)
                ge(dve, pairs_done, s)
                dve.tensor_copy(sums[:, 0:INPUTS * INPUTS].rearrange("p (i j) -> p i j", j=INPUTS),
                                turned[:, :, 0:INPUTS]).then_inc(sums_done, 1)
                v = turned[:, 0, 0:APART]
                above = bass.AP(v.tensor, v.offset + APART + 1, [v.ap[0], (QUAD + 1, APART)])
                dve.tensor_copy(sums[:, INPUTS * INPUTS:], above).then_inc(sums_done, 1)
                choose_pairs(s)

            def pair_products(g, s):
                n = SUBS * g + s
                dve.wait_ge(half_sums, SLICES_SUB * (n + 1 - SUBS))
                dve.wait_ge(sums_done, 2 * n)
                dve.transpose(turned[:, :, :], grams[:, :, :].rearrange("p g m -> p m g")).then_inc(turned_done, 1)
                dve.wait_ge(turned_done, n + 1)
                dve.wait_ge(pairs_done, n)
                full = turned[:, :, 0:INPUTS]
                dve.tensor_tensor(sums[:, 0:INPUTS * INPUTS].rearrange("p (i j) -> p i j", j=INPUTS),
                                  full, full.rearrange("p i j -> p j i"), ALU.add).then_inc(sums_done, 1)
                v = turned[:, 0, 0:APART]
                above = bass.AP(v.tensor, v.offset + APART + 1, [v.ap[0], (QUAD + 1, APART)])
                below = bass.AP(v.tensor, v.offset + QUAD * (APART + 1), [v.ap[0], (QUAD + 1, APART)])
                dve.tensor_tensor(sums[:, INPUTS * INPUTS:], above, below, ALU.add).then_inc(sums_done, 1)
                choose_pairs(n)

            def half_point(g, h):
                p = h // 2
                if h % 2 == 0:
                    if p + XSLOTS - 1 < SLICES:
                        input_hi(g, p + XSLOTS - 1)
                else:
                    half_sum(g, p)
                    if p % SLICES_SUB == SLICES_SUB - 1:
                        pair_products(g, p // SLICES_SUB)

            def pairs_lo_part(g, s, first=False):
                dve.wait_ge(pairs_hi, SUBS * g + s + 1)
                at = slice(s * SUB, (s + 1) * SUB)
                src = pair_bank(first)[0:PAIRS_TILE, 0:PAIR_TILES * SUB].rearrange("p (t b) -> p t b", b=SUB)
                dve.tensor_tensor(featL[0:PAIRS_TILE, 1:KT0, at], src, featH[0:PAIRS_TILE, 1:KT0, at].bitcast(f32),
                                  ALU.subtract).then_inc(pairs_lo, 1)

            def split(c, layer, m, hi, lo, more=True):
                n, cols = nth(c, layer, m, more), columns(c) if layer == 0 else slice(0, CHUNK)
                full, hi, lo = act_out[:, slot(layer, m, more), cols], hi[:, cols], lo[:, cols]
                dve.wait_ge(relu_done, n + 1)
                dve.tensor_copy(hi, full).then_inc(hi_done, 1)
                dve.wait_ge(hi_done, n + 1)
                dve.tensor_tensor(lo, full, hi.bitcast(f32), ALU.subtract).then_inc(split_done, 1)

            def split_left(m):
                full, hi, lo = act_out[:, m % 2, LEFT], h1h[:, m, LEFT], h1l[:, m, LEFT]
                dve.wait_ge(left_relu, m + 1)
                dve.tensor_copy(hi, full).then_inc(left_hi, 1)
                dve.wait_ge(left_hi, m + 1)
                dve.tensor_tensor(lo, full, hi.bitcast(f32), ALU.subtract).then_inc(left_split, 1)

            def pad_input(p):
                dve.wait_ge(x_in[p % XSLOTS], 16 * (p // XSLOTS + 1))
                ge(dve, gram_done, 2 * (p - 2 * XSLOTS + 1))
                dve.tensor_copy(xpad[:, p % (2 * XSLOTS), :, 0:INPUTS], by_sample(xraw, p)).then_inc(xpad_done, 1)

            dve.memset(featH[:, KT0 - 1, :].bitcast(f32), 0.0).then_inc(zero_done, 1)
            dve.memset(featL[:, KT0 - 1, :].bitcast(f32), 0.0).then_inc(zero_done, 1)
            dve.wait_ge(zero_done, 2)
            dve.wait_ge(xpads_zero, XSLOTS)
            for p in range(PAD_AHEAD):
                pad_input(p)
            dve.wait_ge(w4_hi, 1)
            dve.tensor_tensor(w4s[:, :, 1:2], w4raw[:, :, :], w4s[:, :, 0:1].bitcast(f32), ALU.subtract)\
               .then_inc(w4_done, 1)
            for p in range(SLICES):
                if p > TRANSPOSE_AT and (p - TRANSPOSE_AT) % SLICES_SUB == 1:
                    pairs_lo_part(0, (p - TRANSPOSE_AT) // SLICES_SUB, True)
                if p > LEFT_AT:
                    split_left(p - LEFT_AT - 1)
                if p + PAD_AHEAD < SLICES:
                    pad_input(p + PAD_AHEAD)
                if p >= SLICES_SUB and p % SLICES_SUB == 0:
                    first_pairs(p // SLICES_SUB - 1)
                if p == LEFT_AT - 2:
                    dense_parts(0)
            first_pairs(SUBS - 1)
            for m in range(LEFT_AFTER - 1, MT0 - 2):
                split_left(m)
            pairs_lo_part(0, SUBS - 1, True)
            for m in range(MT0 - 2, MT0):
                split_left(m)
            for p in range(XSLOTS - 1):
                input_hi(1, p)

            def body(c, more):
                def on_half(h):
                    if more:
                        half_point(c + 1, h)

                def on_turn(s):
                    if more:
                        pairs_lo_part(c + 1, s)

                def on_tile(layer, m):
                    if layer == 0:
                        split(c, 0, m, h1h[:, m, :], h1l[:, m, :])
                        if more and m < EARLY + XSLOTS - 1 and not at_first(c):
                            input_hi(c + 1, m - EARLY)
                    else:
                        split(c, 1, m, h2h[:, m % 2, :], h2l[:, m % 2, :])

                def after_tile(m):
                    if more and m == 0:
                        dense_parts(c + 1)

                interleave(on_half, on_turn, on_tile, after_tile)
                for m in range(MT2):
                    split(c, 2, m, h1h[:, H3 + m, :], h1l[:, H3 + m, :])
                if more:
                    split(c + 1, 0, 0, h1h[:, 0, :], h1l[:, 0, :])
                for m in range(MT3):
                    split(c, 3, m, h2h[:, m, :], h2l[:, m, :], more)
                if more:
                    split(c + 1, 0, 1, h1h[:, 1, :], h1l[:, 1, :])
                dve.wait_ge(logits_done, c + 1)
                dve.tensor_reduce(ysum[:, :], acc[:, 3, 0:2 * SUBS].rearrange("p (s t) -> p s t", t=2),
                                  mybir.AxisListType.X, ALU.add).then_inc(ysum_done, 1)
                dve.wait_ge(ysum_done, c + 1)
                at = slice(c * SUBS, (c + 1) * SUBS) if isinstance(c, int) else bass.ts(c, SUBS)
                dve.tensor_scalar(y[:, at], ysum[:, :], bias4[:, 0:1], None, ALU.add).then_inc(y_done, 1)

            for m in range(EARLY):
                split(0, 0, m, h1h[:, m, :], h1l[:, m, :])
            body(0, True)
            with dve.Fori(1, CHUNKS - 1) as c:
                body(c, True)
            body(CHUNKS - 1, False)

        @block.tensor
        def _(pe):
            def product(dst, wh, wl, ah, al, start, stop):
                pe.matmul(dst, wl, ah, start=start, stop=False)
                pe.matmul(dst, wh, ah, start=False, stop=False)
                return pe.matmul(dst, wh, al, start=False, stop=stop)

            def first_gram(p):
                pe.wait_ge(xpad_done, p + 1)
                ge(pe, grams_out, 2 * (p - 1))
                for k in range(SLICE_GROUPS):
                    four = xpad[:, p % (2 * XSLOTS), k * GROUP:(k + 1) * GROUP, :]
                    at = k % HALF_GROUPS * GROUP * INPUTS
                    last = pe.matmul(first_banks(p)[:, k // HALF_GROUPS, at:at + GROUP * INPUTS],
                                     four.rearrange("p b n -> p (b n)"), four[:, :, 0:INPUTS], start=True, stop=True)
                last.then_inc(gram_done, 2)

            def gram_half(g, h, turned_before):
                n, p = HALVES * g + h, h // 2
                pe.wait_ge(xh_done, parts(g, p))
                pe.wait_ge(xl_done, parts(g, p))
                pe.wait_ge(grams_out, n)
                pe.wait_ge(pairs_lo, SUBS * g + turned_before)
                for j in range(HALF_GROUPS):
                    k = h % 2 * HALF_GROUPS + j
                    four = slice(k * GROUP, (k + 1) * GROUP)
                    last = pe.matmul(gps[:, j // 2, j % 2 * 2 * P:(j % 2 + 1) * 2 * P],
                                     xs[:, p % XSLOTS, 0, four, :].rearrange("p b n -> p (b n)"),
                                     xs[:, p % XSLOTS, :, four, :].rearrange("p t b n -> p t (b n)"),
                                     start=True, stop=True)
                last.then_inc(gram_done, 1)

            def transpose_pairs(g, s, halves_before, first=False):
                pe.wait_ge(pairs_done, SUBS * g + s + 1)
                if first:
                    ge(pe, pairs_lo, s)
                else:
                    pe.wait_ge(grams_out, HALVES * g + halves_before)
                for t in range(PAIR_TILES):
                    last = pe.transpose(pair_bank(first)[0:PAIRS_TILE, t * SUB:(t + 1) * SUB],
                                        pairs[:, t * PAIRS_TILE:(t + 1) * PAIRS_TILE], ident[:, :])
                last.then_inc(pairs_t, 1)

            def layer0_products(m, samples):
                cols = slice(m * P, (m + 1) * P)
                for k in range(KT0):
                    rows = slice(0, P if k == 0 else PAIRS_TILE if k < KT0 - 1 else ZERO_ROW + 1)
                    last = product(work[:, m % 2, samples], w0h[rows, k, cols], w0l[rows, k, cols],
                                   featH[rows, k, samples], featL[rows, k, samples], k == 0, k == KT0 - 1)
                return last

            def layer0_left(m):
                if m == 0:
                    pe.wait_ge(w0_done, W0_LOADS)
                    pe.wait_ge(dense_done, 1)
                    pe.wait_ge(pairs_lo, SUBS // 2)
                ge(pe, left_relu, m - 1)
                layer0_products(m, LEFT).then_inc(left_done, 1)

            def layer0(c, m):
                if m == 0:
                    pe.wait_ge(dense_done, c + 1)
                    pe.wait_ge(pairs_lo, SUBS * (c + 1))
                if at_first(c) and m < EARLY:
                    pe.wait_ge(left_relu, MT0 - 1 + m)
                if m >= EARLY:
                    pe.wait_ge(relu_done, nth(c, 0, m) - 1)
                layer0_products(m, columns(c)).then_inc(tile_done, 1)

            def layer1(c, m, k):
                if k == 0:
                    pe.wait_ge(w_done, REST + MT1 * c + m + 1)
                    pe.wait_ge(relu_done, nth(c, 1, m) - 1)
                if m == 0 and at_first(c):
                    pe.wait_ge(left_split, k + 1)
                if m == 0:
                    pe.wait_ge(split_done, nth(c, 0, max(k, EARLY)) + (k >= EARLY))
                cols = slice(k * P, (k + 1) * P)
                last = product(work[:, m % 2, :], w1h[:, m % 2, cols], w1l[:, m % 2, cols],
                               h1h[:, k, :], h1l[:, k, :], k == 0, k == KT1 - 1)
                if k == KT1 - 1:
                    last.then_inc(tile_done, 1)

            def layer2(c, k, ms):
                pe.wait_ge(split_done, nth(c, 1, k) + 1)
                for m in ms:
                    cols = slice(k * SIZES[2] + m * P, k * SIZES[2] + (m + 1) * P)
                    last = product(acc[:, m, :], w2h[:, cols], w2l[:, cols], h2h[:, k % 2, :], h2l[:, k % 2, :],
                                   k == 0, k == KT2 - 1)
                    if k == KT2 - 1:
                        last.then_inc(tile_done, 1)

            def layer3(c, m):
                for k in range(KT3):
                    if m == 0:
                        pe.wait_ge(split_done, nth(c, 2, k) + 1)
                    cols = slice(k * SIZES[3] + m * P, k * SIZES[3] + (m + 1) * P)
                    last = product(acc[:, m, :], w3h[:, cols], w3l[:, cols], h1h[:, H3 + k, :], h1l[:, H3 + k, :],
                                   k == 0, k == KT3 - 1)
                last.then_inc(tile_done, 1)

            def layer4(c, more):
                pe.wait_ge(w4_done, 1)
                pe.wait_ge(split_done, nth(c, 3, MT3 - 1, more) + 1)
                for s in range(SUBS):
                    for k in range(MT3):
                        at = slice(s * SUB, (s + 1) * SUB)
                        dst = acc[:, 3, 2 * s:2 * s + 2]
                        pe.matmul(dst, h2h[:, k, at], w4s[:, k, :], start=k == 0, stop=False)
                        last = pe.matmul(dst, h2l[:, k, at], w4s[:, k, :], start=False, stop=k == MT3 - 1)
                last.then_inc(logits_done, 1)

            pe.wait_ge(ident_done, 1)
            for p in range(SLICES):
                first_gram(p)
                if p >= TRANSPOSE_AT and (p - TRANSPOSE_AT) % SLICES_SUB == 0:
                    transpose_pairs(0, (p - TRANSPOSE_AT) // SLICES_SUB, 0, True)
                if p >= LEFT_AT:
                    layer0_left(p - LEFT_AT)
            for m in range(LEFT_AFTER, MT0 - 1):
                layer0_left(m)
            transpose_pairs(0, SUBS - 1, 0, True)
            layer0_left(MT0 - 1)

            for m in range(EARLY):
                layer0(0, m)

            def body(c, more):
                for m in range(EARLY, MT0):
                    layer0(c, m)
                    if m == FIRST_HALF:
                        pe.wait_ge(pads_done, XSLOTS)
                    if more and m >= FIRST_HALF:
                        gram_half(c + 1, m - FIRST_HALF, 0)
                for m in range(MT1):
                    for k in range(KT1):
                        layer1(c, m, k)
                        if more and (m, k) in IN_L1:
                            gram_half(c + 1, IN_L1[m, k], before((m, k))[1])
                        if more and (m, k) in TURNS:
                            transpose_pairs(c + 1, TURNS[m, k], before((m, k))[0])
                    if m:
                        if m == 1:
                            pe.wait_ge(w_done, W2_LOADS)
                        layer2(c, m - 1, range(MT2 // 2))
                        if more and (m, KT1) in IN_L1:
                            gram_half(c + 1, IN_L1[m, KT1], before((m, KT1))[1])
                        if more and (m, KT1) in TURNS:
                            transpose_pairs(c + 1, TURNS[m, KT1], before((m, KT1))[0])
                        layer2(c, m - 1, range(MT2 // 2, MT2))
                layer2(c, KT2 - 1, range(MT2))
                if more:
                    layer0(c + 1, 0)
                pe.wait_ge(w_done, REST)
                for m in range(MT3):
                    layer3(c, m)
                if more:
                    layer0(c + 1, 1)
                layer4(c, more)

            body(0, True)
            with pe.Fori(1, CHUNKS - 1) as c:
                body(c, True)
            body(CHUNKS - 1, False)


def kernel(**inputs):
    import concourse.bacc as _bacc
    from concourse.bass_utils import run_bass_kernel_spmd as _run

    x = np.ascontiguousarray(inputs["r_bottom_output"])
    W = [np.ascontiguousarray(inputs[f"L0_rec_W{i}"]) for i in range(5)]
    b = [np.ascontiguousarray(inputs[f"L0_rec_b{i}"]) for i in range(5)]

    xs = x.reshape(GROUP, QUAD, CHUNKS * SUBS, INPUTS, EMB)
    x_t = xs.transpose(2, 1, 0, 3, 4).reshape(CHUNKS * SLICES, SLICE_GROUPS * GROUP * INPUTS, EMB).transpose(0, 2, 1)
    x0_t = x[:, 0, :].reshape(P, CHUNKS, SUBS, EMB).transpose(1, 3, 2, 0).reshape(CHUNKS, EMB, CHUNK)

    rows = pair_features()
    w0 = np.zeros((KT0, P, SIZES[0]), W[0].dtype)
    w0[rows >= 0] = W[0].T[rows[rows >= 0]]
    w1 = W[1].reshape(MT1, P, KT1, P).transpose(0, 3, 2, 1).reshape(MT1, P, KT1 * P)
    w2 = W[2].T.reshape(KT2, P, SIZES[2]).transpose(1, 0, 2).reshape(P, W2_LOADS, LOAD).transpose(1, 0, 2)
    w3 = W[3].T.reshape(KT3, P, SIZES[3]).transpose(1, 0, 2).reshape(P, KT3 * SIZES[3])
    w4 = W[4].reshape(MT3, P, 1).transpose(1, 0, 2)
    biases = np.concatenate([v.reshape(-1, P) for v in b[:4]]).T

    nc = _bacc.Bacc("TRN2", target_bir_lowering=False, num_devices=1, dynamic_dma_scratch_size=1024)
    arrays = {}

    def given(name, a):
        arrays[name] = np.ascontiguousarray(a)
        return nc.dram_tensor(name, arrays[name].shape, mybir.dt.from_np(a.dtype), kind="ExternalInput").ap()

    args = [given("x_t", x_t), given("x0_t", x0_t), given("w0_t", w0), given("w1_t", w1), given("w2_t", w2),
            given("w3_t", w3), given("w4_t", w4), given("biases", biases), given("b4", b[4].reshape(1, 1))]
    out = nc.dram_tensor("out_0", (BATCH, 1), mybir.dt.float32, kind="ExternalOutput").ap()
    rec_program(nc, *args, out.rearrange("(p t) a -> p (t a)", p=P))
    r = _run(nc, [arrays], core_ids=[0])
    return r.results[0]["out_0"]
```
